# Optimizing a Trainium2 kernel written in Bass

```python
import numpy as np
import jax
import jax.numpy as jnp

def _softmax(x, axis=-1):
    return jax.nn.softmax(x, axis=axis)

def _gelu(x):
    return jax.nn.gelu(x, approximate=True)

def _silu(x):
    return jax.nn.silu(x)

def _sigmoid(x):
    return jax.nn.sigmoid(x)

def _layernorm(x, axis=-1, eps=1e-05):
    m = jnp.mean(x, axis=axis, keepdims=True)
    v = jnp.var(x, axis=axis, keepdims=True)
    return (x - m) / jnp.sqrt(v + eps)

def _scatter_add(tgt, idx, src, axis=0):
    return tgt.at[idx].add(src)

def _segment_sum(src, seg, n):
    return jax.ops.segment_sum(src, seg, n)
kernel_name = 'mk_adj_preln_d2_adj_r2_2d1a14'

def setup_inputs(seed: int=0):
    np.random.seed(seed)
    _w = jnp.asarray

    def _rec_inputs():
        import jax
        import jax.numpy as jnp
        _gk = jax.random.key(seed)
        x = -0.0002928 + 1 * jax.random.normal(jax.random.fold_in(_gk, 1), (2048, 512), jnp.float32)
        _w = (1.0 + jnp.arange(2048, dtype=jnp.float32)) ** (-0.5)
        _w = _w / _w.mean()
        _pij = jnp.clip(0.000976562 * _w[:, None] * _w[None, :], 0.0, 1.0)
        _a = jax.random.uniform(jax.random.fold_in(_gk, 2), (2048, 2048)) < _pij
        _af = _a.astype(jnp.float32)
        adj = _af
        return (x, adj)
    x, adj = _rec_inputs()

    def _L0_gnn_setup():
        import jax, jax.numpy as jnp
        import numpy as np
        N = 2048
        D_IN = 512
        H = 16
        DH = D_IN // H
        ALPHA = 0.2
        MASK_VAL = -65500.0
        key = jax.random.key(seed)
        ks = jax.random.split(key, 7)
        x = jax.random.normal(ks[0], (N, D_IN), dtype=jnp.float32)
        adj = jax.random.randint(ks[1], (N, N), 0, 2).astype(jnp.float32)
        s = 1.0 / np.sqrt(D_IN)
        W_seq = jax.random.normal(ks[2], (D_IN, D_IN), dtype=jnp.float32) * s
        a1 = jax.random.normal(ks[3], (DH,), dtype=jnp.float32) / np.sqrt(DH)
        a2 = jax.random.normal(ks[4], (DH,), dtype=jnp.float32) / np.sqrt(DH)
        W_out = jax.random.normal(ks[5], (D_IN, D_IN), dtype=jnp.float32) * s
        b_out = jax.random.normal(ks[6], (D_IN,), dtype=jnp.float32) * 0.01
        return {'x': x, 'adj': adj, 'W_seq': W_seq, 'a1': a1, 'a2': a2, 'W_out': W_out, 'b_out': b_out}
    _L0_gnn_all = _L0_gnn_setup()
    _L0_gnn_in = {k: v for k, v in _L0_gnn_all.items() if k in ('W_seq', 'a1', 'a2', 'W_out', 'b_out')}
    del _L0_gnn_all

    def _L1_gnn_setup():
        import jax, jax.numpy as jnp
        import numpy as np
        ALPHA = 0.2
        NEG = -9000000000000000.0
        N, NFEAT, NHID, NHEADS = (2048, 512, 64, 8)
        EMB = NHID * NHEADS
        key = jax.random.key(seed)
        ks = jax.random.split(key, 16)
        x = jax.random.normal(ks[0], (N, NFEAT), dtype=jnp.float32)
        adj = (jax.random.uniform(ks[1], (N, N)) < 0.01).astype(jnp.float32)
        adj = jnp.maximum(adj, jnp.eye(N, dtype=jnp.float32))
        s = 0.05
        W = jax.random.normal(ks[2], (NHEADS, NFEAT, NHID), dtype=jnp.float32) * s
        a1 = jax.random.normal(ks[3], (NHEADS, NHID), dtype=jnp.float32) * s
        a2 = jax.random.normal(ks[4], (NHEADS, NHID), dtype=jnp.float32) * s
        W1 = jax.random.normal(ks[5], (EMB // 2, EMB), dtype=jnp.float32) * s
        b1 = jnp.zeros((EMB // 2,), dtype=jnp.float32)
        W2 = jax.random.normal(ks[6], (NFEAT // 4, EMB // 2), dtype=jnp.float32) * s
        b2 = jnp.zeros((NFEAT // 4,), dtype=jnp.float32)
        W3 = jax.random.normal(ks[7], (NFEAT // 2, NFEAT // 4), dtype=jnp.float32) * s
        b3 = jnp.zeros((NFEAT // 2,), dtype=jnp.float32)
        W4 = jax.random.normal(ks[8], (NFEAT, NFEAT // 2), dtype=jnp.float32) * s
        b4 = jnp.zeros((NFEAT,), dtype=jnp.float32)
        return {'x': x, 'adj': adj, 'W': W, 'a1': a1, 'a2': a2, 'W1': W1, 'b1': b1, 'W2': W2, 'b2': b2, 'W3': W3, 'b3': b3, 'W4': W4, 'b4': b4}
    _L1_gnn_all = _L1_gnn_setup()
    _L1_gnn_in = {k: v for k, v in _L1_gnn_all.items() if k in ('W', 'a1', 'a2', 'W1', 'b1', 'W2', 'b2', 'W3', 'b3', 'W4', 'b4')}
    del _L1_gnn_all
    return {'x': x, 'adj': adj, 'L0_gnn_W_seq': _L0_gnn_in['W_seq'], 'L0_gnn_a1': _L0_gnn_in['a1'], 'L0_gnn_a2': _L0_gnn_in['a2'], 'L0_gnn_W_out': _L0_gnn_in['W_out'], 'L0_gnn_b_out': _L0_gnn_in['b_out'], 'L1_gnn_W': _L1_gnn_in['W'], 'L1_gnn_a1': _L1_gnn_in['a1'], 'L1_gnn_a2': _L1_gnn_in['a2'], 'L1_gnn_W1': _L1_gnn_in['W1'], 'L1_gnn_b1': _L1_gnn_in['b1'], 'L1_gnn_W2': _L1_gnn_in['W2'], 'L1_gnn_b2': _L1_gnn_in['b2'], 'L1_gnn_W3': _L1_gnn_in['W3'], 'L1_gnn_b3': _L1_gnn_in['b3'], 'L1_gnn_W4': _L1_gnn_in['W4'], 'L1_gnn_b4': _L1_gnn_in['b4']}

def reference(x, adj, L0_gnn_W_seq, L0_gnn_a1, L0_gnn_a2, L0_gnn_W_out, L0_gnn_b_out, L1_gnn_W, L1_gnn_a1, L1_gnn_a2, L1_gnn_W1, L1_gnn_b1, L1_gnn_W2, L1_gnn_b2, L1_gnn_W3, L1_gnn_b3, L1_gnn_W4, L1_gnn_b4):
    import jax
    import jax.numpy as jnp

    def _L0_gnn_ref(x, adj, W_seq, a1, a2, W_out, b_out):
        import jax, jax.numpy as jnp
        import numpy as np
        N = 2048
        D_IN = 512
        H = 16
        DH = D_IN // H
        ALPHA = 0.2
        MASK_VAL = -65500.0
        seq = (x @ W_seq).reshape(N, H, DH)
        score1 = jnp.einsum('nhd,d->hn', seq, a1)
        score2 = jnp.einsum('nhd,d->hn', seq, a2)
        scores = score1[:, :, None] + score2[:, None, :]
        scores = jax.nn.leaky_relu(scores, negative_slope=ALPHA)
        scores = scores + (1.0 - adj)[None, :, :] * MASK_VAL
        attn = jax.nn.softmax(scores, axis=-1)
        hidden = jnp.einsum('hij,jhd->ihd', attn, seq).reshape(N, D_IN)
        hidden = hidden @ W_out + b_out
        return jax.nn.elu(hidden)

    def _L1_gnn_ref(x, adj, W, a1, a2, W1, b1, W2, b2, W3, b3, W4, b4):
        import jax, jax.numpy as jnp
        import numpy as np
        ALPHA = 0.2
        NEG = -9000000000000000.0
        N, NFEAT, NHID, NHEADS = (2048, 512, 64, 8)
        EMB = NHID * NHEADS
        Wh = jnp.einsum('nf,hfd->hnd', x, W)
        e_src = jnp.einsum('hnd,hd->hn', Wh, a1)
        e_dst = jnp.einsum('hnd,hd->hn', Wh, a2)
        e = jax.nn.leaky_relu(e_src[:, :, None] + e_dst[:, None, :], ALPHA)
        e = jnp.where(adj[None] > 0, e, NEG)
        att = jax.nn.softmax(e, axis=-1)
        h = jnp.einsum('hnm,hmd->hnd', att, Wh)
        h = jax.nn.elu(h)
        enc = jnp.transpose(h, (1, 0, 2)).reshape(x.shape[0], -1)
        out = jax.nn.relu(enc @ W1.T + b1)
        out = jax.nn.relu(out @ W2.T + b2)
        out = jax.nn.relu(out @ W3.T + b3)
        out = out @ W4.T + b4
        return out
    h = jnp.maximum(_layernorm(x, axis=-1), 0.0)
    x = x + _L0_gnn_ref(h, adj, L0_gnn_W_seq, L0_gnn_a1, L0_gnn_a2, L0_gnn_W_out, L0_gnn_b_out)
    h = jnp.maximum(_layernorm(x, axis=-1), 0.0)
    x = x + _L1_gnn_ref(h, adj, L1_gnn_W, L1_gnn_a1, L1_gnn_a2, L1_gnn_W1, L1_gnn_b1, L1_gnn_W2, L1_gnn_b2, L1_gnn_W3, L1_gnn_b3, L1_gnn_W4, L1_gnn_b4)
    return x

_drawn_inputs = setup_inputs


def setup_inputs(seed=0):
    import zlib

    import numpy as np

    out = dict(_drawn_inputs(seed))
    spreads = {'L1_gnn_b1': (0.0, 0.677),
     'L1_gnn_b2': (0.0, 0.369),
     'L1_gnn_b3': (0.0, 0.1),
     'L1_gnn_b4': (0.0, 0.1)}
    factors = {'L0_gnn_a1': 2.681, 'L0_gnn_b_out': 7.033, 'L1_gnn_a1': 64.0, 'L1_gnn_a2': 22.027}
    for name, (base, spread) in spreads.items():
        noise = np.random.default_rng([zlib.crc32(name.encode()), seed]).standard_normal(out[name].shape)
        drawn = base * np.exp(spread * noise) if base else spread * noise
        out[name] = jnp.asarray(drawn.astype(out[name].dtype))
    for name, factor in factors.items():
        out[name] = (out[name] * factor).astype(out[name].dtype)
    return out
```

```python
import concourse.bass as bass
from concourse import mybir
from contextlib import ExitStack

fp32 = mybir.dt.float32
bf16 = mybir.dt.bfloat16
fp8 = mybir.dt.float8e4
u8 = mybir.dt.uint8
i8 = mybir.dt.int8
u16 = mybir.dt.uint16
ALU = mybir.AluOpType
ACT = mybir.ActivationFunctionType
AX = mybir.AxisListType
RMAX = bass.bass_isa.ReduceOp.max

P = 128
N = 2048
F = 512
NT = N // P
KT = F // P
HALF = N // 2
CH = 4
NC = NT // CH
ONE8 = 56
S2 = 16
SC = 32
LIFT = 60.0
SLOPE = 0.2
EPS = 1e-5


def rows(it, n=P):
    return slice(it * n, (it + 1) * n) if isinstance(it, int) else bass.ds(it * n, n)


def wait_from(eng, sem, value):
    if not isinstance(value, int) or value > 0:
        eng.wait_ge(sem, value)


def tile_pairs(eng, body):
    for b in range(2):
        body(b, b)
    with eng.Fori(1, NT // 2 - 1) as m:
        for b in range(2):
            body(2 * m + b, b)
    for b in range(2):
        body(NT - 2 + b, b)


def attention(nc, tag, H, D, dve_tiles, mask, v, bd, ratio, neg_s2, s1_rows, t_buf, u_buf, s1,
              parts, shift, sums, ps, sem, empty=None):
    D1 = D + 1
    W3 = 3 * D1
    PAIRS = H // 2
    act_tiles = [jt for jt in range(NT) if jt not in dve_tiles]
    NA, ND = len(act_tiles), len(dve_tiles)

    s1_loaded = [sem(f"{tag}_s1_loaded{b}") for b in range(2)]
    act_shift = sem(tag + "_act_shift")
    dve_shift = sem(tag + "_dve_shift")
    group_begun = sem(tag + "_group_begun")
    act_compared = sem(tag + "_act_compared")
    dve_compared = sem(tag + "_dve_compared")
    t_ready = sem(tag + "_t_ready")
    u_ready = sem(tag + "_u_ready")
    weighted = sem(tag + "_weighted")
    parts_ready = sem(tag + "_parts_ready")
    group_done = sem(tag + "_group_done")
    group_free = sem(tag + "_group_free")
    post = sem(tag + "_post")

    filled = sem(tag + "_filled")

    with nc.Block() as block:

        @block.sync
        def _(sp):
            def load(h, b):
                sp.dma_start(s1[:, b, :], s1_rows[h:h + 1, :].rearrange("a n -> (a n)").partition_broadcast(P)
                             if isinstance(h, int) else
                             s1_rows[bass.ds(h, 1), :].rearrange("a n -> (a n)").partition_broadcast(P)
                             ).then_inc(s1_loaded[b], 16)

            load(0, 0)
            load(1, 1)
            with sp.Fori(1, PAIRS) as m:
                for b in range(2):
                    sp.wait_ge(act_compared, 4 * NA * m + 2 * NA * b - 2 * NA)
                    if ND:
                        sp.wait_ge(dve_compared, 4 * ND * m + 2 * ND * b - 2 * ND)
                    load(2 * m + b, b)

        @block.scalar
        def _(act):
            with act.Fori(0, PAIRS) as m:
                for k in range(4):
                    b, half = k // 2, k % 2
                    if half == 0:
                        act.activation(shift[:, 0, b, :].unsqueeze(2), neg_s2[:, :, bass.ds(2 * m + b, 1)],
                                       ACT.Copy).then_inc(act_shift, 1)
                        act.wait_ge(act_shift, 2 * m + b + 1)
                        act.wait_ge(s1_loaded[b], 16 * m + 16)
                    act.wait_ge(group_done, 8 * m + 2 * k + 2)
                    for jt in act_tiles:
                        act.activation(t_buf[:, half, jt, :].bitcast(i8), s1[:, b, half * HALF:(half + 1) * HALF],
                                       ACT.Sign, bias=shift[:, 0, b, jt:jt + 1],
                                       scale=-1.0).then_inc(act_compared, 1)

        @block.vector
        def _(dve):
            def split_values(m, b):
                h = 2 * m + b
                w = parts[:, b, :, :, :, :]
                src = v[:, :, h * D1:(h + 1) * D1] if isinstance(m, int) else v[:, :, bass.ds(h * D1, D1)]
                for x in range(2):
                    f = bd[:, x, :, h:h + 1] if isinstance(m, int) else bd[:, x, :, bass.ds(h, 1)]
                    nc.vector.tensor_tensor(w[:, x, :, :, 0], src,
                                            f.to_broadcast([P, NT, D1]), ALU.mult).then_inc(weighted, 1)
                for c in range(1, 3):
                    for x in range(2):
                        dve.wait_ge(weighted, 6 * h + 2 * (c - 1) + x + 1)
                        whole = w[:, x, :, :, c - 1]
                        nc.vector.tensor_tensor(
                            w[:, x, :, :, c], whole,
                            w[:, x, :, :, :].bitcast(bf16)[:, :, :, 2 * c - 1],
                            ALU.subtract).then_inc(weighted, 1)
                dve.wait_ge(weighted, 6 * h + 6)
                dve.sem_inc(parts_ready, 1)

            def take_shift(m, b):
                if not ND:
                    return
                h = 2 * m + b
                hs = slice(h, h + 1) if isinstance(m, int) else bass.ds(h, 1)
                nc.vector.tensor_copy(shift[:, 1, b, :].unsqueeze(2), neg_s2[:, :, hs]).then_inc(dve_shift, 1)
                dve.wait_ge(dve_shift, h + 1)

            def compare(m, k):
                b, half = k // 2, k % 2
                if not ND:
                    return
                if half == 0:
                    dve.wait_ge(s1_loaded[b], 16 * m + 16)
                dve.wait_ge(group_done, 8 * m + 2 * k + 2)
                for jt in dve_tiles:
                    nc.vector.tensor_scalar(t_buf[:, half, jt, :], s1[:, b, half * HALF:(half + 1) * HALF],
                                            shift[:, 1, b, jt:jt + 1], float(ONE8), ALU.is_gt, ALU.mult).then_inc(dve_compared, 1)

            def masks(m, k, c):
                half = k % 2
                jts = slice(c * CH, (c + 1) * CH)
                words = lambda ap: ap.bitcast(u16)
                t = words(t_buf[:, half, jts, :])
                mk = words(mask[:, jts, half * HALF:(half + 1) * HALF])
                na = sum(jt < (c + 1) * CH for jt in act_tiles)
                nd = sum(jt < (c + 1) * CH for jt in dve_tiles)
                dve.wait_ge(act_compared, (4 * m + k) * NA + na)
                if nd:
                    dve.wait_ge(dve_compared, (4 * m + k) * ND + nd)
                nc.vector.tensor_tensor(t, t, mk, ALU.bitwise_and).then_inc(t_ready, 1)

            def rest(m, k, c):
                half = k % 2
                jts = slice(c * CH, (c + 1) * CH)
                words = lambda ap: ap.bitcast(u16)
                dve.wait_ge(t_ready, (4 * m + k) * NC + c + 1)
                nc.vector.tensor_tensor(words(u_buf[:, half, jts, :]), words(t_buf[:, half, jts, :]),
                                        words(mask[:, jts, half * HALF:(half + 1) * HALF]),
                                        ALU.bitwise_xor).then_inc(u_ready, 1)

            def drain(n, slot4, half, g):
                dve.wait_ge(group_done, n + 5)
                it = half * (NT // 2) + 4 * g
                nc.vector.tensor_reduce(sums[:, it:it + 4, :],
                                        ps[:, 4 * g:4 * g + 4, 0:2 * W3].rearrange("p k (m c) -> p k m c", c=3),
                                        AX.X, ALU.add).then_inc(group_free, 1)

            def normalise(m, b):
                h = 2 * m + b
                hs = slice(h, h + 1) if isinstance(h, int) else bass.ds(h, 1)
                vs = slice(h * D, h * D + D) if isinstance(h, int) else bass.ds(h * D, D)
                dve.wait_ge(group_free, 4 * h + 6)
                nc.vector.tensor_tensor(sums[:, :, D1:2 * D1], sums[:, :, D1:2 * D1],
                                        ratio[:, :, hs].to_broadcast([P, NT, D1]), ALU.mult).then_inc(post, 1)
                dve.wait_ge(post, 4 * h + 1)
                nc.vector.tensor_tensor(sums[:, :, 0:D1], sums[:, :, 0:D1], sums[:, :, D1:2 * D1],
                                        ALU.add).then_inc(post, 1)
                dve.wait_ge(post, 4 * h + 2)
                if empty is not None:
                    nc.vector.tensor_tensor(sums[:, :, D:D1], sums[:, :, D:D1],
                                            empty[:, :].unsqueeze(2), ALU.add).then_inc(filled, 1)
                    dve.wait_ge(filled, h + 1)
                nc.vector.reciprocal(sums[:, :, D1:D1 + 1], sums[:, :, D:D1]).then_inc(post, 1)
                dve.wait_ge(post, 4 * h + 3)
                nc.vector.tensor_tensor(v[:, :, vs], sums[:, :, 0:D],
                                        sums[:, :, D1:D1 + 1].to_broadcast([P, NT, D]), ALU.mult).then_inc(post, 1)

            def unit(m, k, first=False):
                b, half = k // 2, k % 2
                if half == 0:
                    take_shift(m, b)
                    split_values(m, b)
                compare(m, k)
                before = half != 0 or b != 0 or not first
                pk = (k - 1) % 4
                n = 8 * m + 2 * k - 2
                masks(m, k, 0)
                masks(m, k, 1)
                rest(m, k, 0)
                rest(m, k, 1)
                if before:
                    drain(n, None, pk % 2, 0)
                masks(m, k, 2)
                masks(m, k, 3)
                rest(m, k, 2)
                rest(m, k, 3)
                if before:
                    drain(n + 1, None, pk % 2, 1)
                    if half == 0:
                        normalise(m if b else m - 1, 1 - b)

            dve.sem_inc(group_free, 2)
            for k in range(4):
                unit(0, k, first=(k == 0))
            with dve.Fori(1, PAIRS) as m:
                for k in range(4):
                    unit(m, k)
            drain(4 * H - 2, None, 1, 0)
            drain(4 * H - 1, None, 1, 1)
            normalise(PAIRS - 1, 1)

        @block.tensor
        def _(pe):
            pe.sem_inc(group_done, 4)
            with pe.Fori(0, PAIRS) as m:
                for k in range(4):
                    b, half = k // 2, k % 2
                    if half == 0:
                        pe.wait_ge(parts_ready, 2 * m + b + 1)
                    pe.wait_ge(u_ready, 4 * NC * m + NC * (k + 1))
                    for g in range(2):
                        pe.wait_ge(group_free, 8 * m + 2 * k + g + 1)
                        pe.sem_inc(group_begun, 1)
                        for q in range(4):
                            it = 4 * g + q
                            for x, side in enumerate((t_buf, u_buf)):
                                for jt in range(NT):
                                    last = nc.tensor.matmul(
                                        ps[:, it, x * W3:(x + 1) * W3],
                                        side[:, half, jt, it * P:(it + 1) * P].bitcast(fp8),
                                        parts[:, b, x, jt, :, :].rearrange("p d c -> p (d c)").bitcast(bf16)[:, 1::2],
                                        start=(jt == 0), stop=(jt == NT - 1))
                        last.then_inc(group_done, 1)


def transform(nc, tag, H, D, HA, x, x_dram, w_dram, a_dram, v, w, a_bc, wa, tmp, xn, hT, stats, mv, sc,
              ident, ps, sem, mask=None, adj=None, adj_dram=None):
    D1 = D + 1
    XCH = 4

    x_loaded = [sem(f"{tag}_x_loaded{c}") for c in range(XCH)]
    w_loaded = sem(tag + "_w_loaded")
    ones_set = sem(tag + "_ones_set")
    wa_step = sem(tag + "_wa_step")
    wa_ready = sem(tag + "_wa_ready")
    stats_ready = sem(tag + "_stats_ready")
    var_ready = sem(tag + "_var_ready")
    dev_ready = sem(tag + "_dev_ready")
    rstd_ready = sem(tag + "_rstd_ready")
    xn_ready = sem(tag + "_xn_ready")
    turned = sem(tag + "_turned")
    hT_ready = sem(tag + "_hT_ready")
    v_summed = sem(tag + "_v_summed")
    s_summed = sem(tag + "_s_summed")
    v_out = sem(tag + "_v_out")
    s_out = sem(tag + "_s_out")
    adj_loaded = [sem(f"{tag}_adj_loaded{b}") for b in range(2)]
    adj_turned = sem(tag + "_adj_turned")
    mask_dve = sem(tag + "_mask_dve")
    mask_act = sem(tag + "_mask_act")

    vh = v.rearrange("p t (h d) -> p t h d", d=D1)

    with nc.Block() as block:

        @block.sync
        def _(sp):
            if x_dram is not None:
                for c in range(XCH):
                    sp.dma_start(x[:, 4 * c:4 * c + 4, :],
                                 x_dram[c * 512:(c + 1) * 512, :].rearrange("(t p) f -> p t f", p=P)
                                 ).then_inc(x_loaded[c], 16)
            if mask is not None:
                def load(it, b):
                    wait_from(sp, adj_turned, 4 * it - 4)
                    sp.dma_start(adj[:, b, :], adj_dram[rows(it), :]).then_inc(adj_loaded[b], 16)
                tile_pairs(sp, load)

        @block.gpsimd
        def _(pool):
            if x_dram is not None:
                nc.gpsimd.memset(ident[:, :], 0.0).then_inc(ones_set, 1)
                pool.wait_ge(ones_set, 1)
                nc.gpsimd.affine_select(out=ident[:, :], in_=ident[:, :], compare_op=ALU.not_equal, fill=1.0,
                                        base=0, pattern=[[-1, P]], channel_multiplier=1).then_inc(ones_set, 1)
            else:
                pool.sem_inc(ones_set, 2)
            nc.gpsimd.memset(wa[:, :, :], 0.0).then_inc(ones_set, 1)
            nc.gpsimd.memset(vh[:, :, :, D:D1], 1.0).then_inc(ones_set, 1)

        @block.scalar
        def _(act):
            for kt in range(KT):
                act.dma_start(w[:, kt, :].rearrange("p (h d) -> p h d", d=D), w_dram[kt]).then_inc(w_loaded, 16)
            for a, src in enumerate(a_dram):
                act.dma_start(a_bc[:, a, :], src.partition_broadcast(P)).then_inc(w_loaded, 16)
            act.wait_ge(var_ready, NT)
            act.activation(mv[:, :, 1:2], mv[:, :, 1:2], ACT.Sqrt, bias=mv[:, 0:1, 2:3].rearrange("p a b -> p (a b)")
                           ).then_inc(dev_ready, 1)

            def copy_v(it, b):
                act.wait_ge(v_summed, it + 1)
                act.activation(vh[:, it if isinstance(it, int) else bass.ds(it, 1), :, 0:D] if isinstance(it, int)
                               else vh[:, bass.ds(it, 1), :, 0:D].rearrange("p a h d -> p (a h) d"),
                               ps[:, 2 + b, :].rearrange("p (h d) -> p h d", d=D), ACT.Copy).then_inc(v_out, 1)

            def copy_mask(it, b, q):
                act.wait_ge(adj_turned, 4 * it + q + 1)
                act.activation(mask[:, 4 * q:4 * q + 4, rows(it)], ps[:, 7, :].rearrange("p (j i) -> p j i", i=P),
                               ACT.Copy, scale=float(ONE8)).then_inc(mask_act, 1)

            def tile(it, b):
                act.wait_ge(turned, it + 1)
                wait_from(act, v_summed, it - 1)
                wait_from(act, s_summed, it - 1)
                act.activation(hT[:, b, :, :], ps[:, b, :].rearrange("p (k i) -> p k i", i=P),
                               ACT.Relu).then_inc(hT_ready, 1)
                if mask is not None:
                    copy_mask(it, b, 1)
                if not isinstance(it, int) or it > 0:
                    copy_v(it - 1, 1 - b)
                if mask is not None:
                    copy_mask(it, b, 3)
            tile_pairs(act, tile)
            copy_v(NT - 1, 1)

        @block.vector
        def _(dve):
            dve.wait_ge(w_loaded, 16 * (KT + 2))
            dve.wait_ge(ones_set, 3)
            step = 0
            for a in range(2):
                vec = a_bc[:, a, :].rearrange("p (h d) -> p h d", d=D)
                if HA == 1:
                    vec = vec.to_broadcast([P, H, D])
                for k in range(KT):
                    prod = tmp[:, k % 2, :].rearrange("p (h d) -> p h d", d=D)
                    nc.vector.tensor_tensor(prod, w[:, k, :].rearrange("p (h d) -> p h d", d=D), vec,
                                            ALU.mult).then_inc(wa_step, 1)
                    step += 1
                    dve.wait_ge(wa_step, step)
                    nc.vector.tensor_reduce(wa[:, k, S2 * a:S2 * a + H], prod, AX.X, ALU.add).then_inc(wa_ready, 1)
            nc.vector.memset(mv[:, :, 2:3], EPS).then_inc(wa_step, 1)
            for c in range(XCH):
                if x_dram is not None:
                    dve.wait_ge(x_loaded[c], 16)
                for it in range(4 * c, 4 * c + 4):
                    nc.vector.bn_stats(stats[:, it, :], x[:, it, :]).then_inc(stats_ready, 1)
            for it in range(NT):
                dve.wait_ge(stats_ready, it + 1)
                nc.vector.bn_aggr(mv[:, it, 0:2], stats[:, it, :]).then_inc(var_ready, 1)
            dve.wait_ge(dev_ready, 1)
            nc.vector.reciprocal(mv[:, :, 1:2], mv[:, :, 1:2]).then_inc(rstd_ready, 1)
            dve.wait_ge(rstd_ready, 1)

            def normalise(it, b):
                wait_from(dve, turned, it - 1)
                src = x[:, it, :] if isinstance(it, int) else x[:, bass.ds(it, 1), :].rearrange("p a f -> p (a f)")
                st = lambda c: (mv[:, it, c:c + 1] if isinstance(it, int)
                                else mv[:, bass.ds(it, 1), c:c + 1].rearrange("p a f -> p (a f)"))
                nc.vector.tensor_scalar(xn[:, b, :], src, st(0), st(1), ALU.subtract, ALU.mult).then_inc(xn_ready, 1)

            def copy_s(it, b):
                dve.wait_ge(s_summed, it + 1)
                dst = sc[:, it, :] if isinstance(it, int) else sc[:, bass.ds(it, 1), :].rearrange("p a f -> p (a f)")
                nc.vector.tensor_copy(dst, ps[:, 4 + b, 0:SC]).then_inc(s_out, 1)

            def copy_mask(it, q):
                dve.wait_ge(adj_turned, 4 * it + q + 1)
                nc.vector.tensor_scalar(mask[:, 4 * q:4 * q + 4, rows(it)],
                                        ps[:, 6, :].rearrange("p (j i) -> p j i", i=P),
                                        float(ONE8), None, ALU.mult).then_inc(mask_dve, 1)

            def tile(it, b):
                if mask is not None:
                    copy_mask(it, 0)
                if not isinstance(it, int) or it < NT - 1:
                    normalise(it + 1, 1 - b)
                if not isinstance(it, int) or it > 0:
                    copy_s(it - 1, 1 - b)
                if mask is not None:
                    copy_mask(it, 2)
            normalise(0, 0)
            tile_pairs(dve, tile)
            copy_s(NT - 1, 1)

        @block.tensor
        def _(pe):
            pe.wait_ge(ones_set, 4)
            pe.wait_ge(w_loaded, 16 * (KT + 2))

            def turn(it, b):
                pe.wait_ge(xn_ready, it + 1)
                wait_from(pe, hT_ready, it - 1)
                for k in range(KT):
                    last = nc.tensor.transpose(ps[:, b, rows(k)], xn[:, b, rows(k)], ident[:, :])
                last.then_inc(turned, 1)

            def turn_adj(it, b, q0):
                if q0 == 0:
                    pe.wait_ge(adj_loaded[b], 8 * (it - b) + 16)
                for q in (q0, q0 + 1):
                    wait_from(pe, (mask_dve, mask_act)[q % 2], 2 * it + q // 2)
                    for j in range(4):
                        last = nc.tensor.transpose(ps[:, 6 + q % 2, rows(j)], adj[:, b, rows(4 * q + j)], ident[:, :])
                    last.then_inc(adj_turned, 1)

            def project(it, b):
                pe.wait_ge(hT_ready, it + 1)
                wait_from(pe, v_out, it - 1)
                for k in range(KT):
                    last = nc.tensor.matmul(ps[:, 2 + b, :], hT[:, b, k, :], w[:, k, :],
                                            start=(k == 0), stop=(k == KT - 1))
                last.then_inc(v_summed, 1)

            def project_scores(it, b):
                if isinstance(it, int) and it == 0:
                    pe.wait_ge(wa_ready, 2 * KT)
                wait_from(pe, s_out, it - 1)
                for k in range(KT):
                    last = nc.tensor.matmul(ps[:, 4 + b, 0:SC], hT[:, b, k, :], wa[:, k, :],
                                            start=(k == 0), stop=(k == KT - 1))
                last.then_inc(s_summed, 1)

            def tile(it, b):
                turn(it, b)
                if mask is not None:
                    turn_adj(it, b, 0)
                if not isinstance(it, int) or it > 0:
                    project(it - 1, 1 - b)
                    project_scores(it - 1, 1 - b)
                if mask is not None:
                    turn_adj(it, b, 2)
            tile_pairs(pe, tile)
            project(NT - 1, 1)
            project_scores(NT - 1, 1)


def factors(nc, tag, H, D, sc, v, sh, zr, gm, g, bd, ratio, neg_s2, s_rows, rows_dram, mask, ones8, e_row, e_byte,
            e_col, mean_w, mean, ident, ps, sem, first):
    D1 = D + 1
    step = sem(tag + "_step")
    max_ready = sem(tag + "_max_ready")
    consts = sem(tag + "_consts")
    shifted = sem(tag + "_shifted")
    exps = sem(tag + "_exps")
    turned = sem(tag + "_turned")
    degrees = sem(tag + "_degrees")
    e_ready = sem(tag + "_e_ready")
    col_done = sem(tag + "_col_done")
    lifted = sem(tag + "_lifted")
    stored = sem(tag + "_stored")

    with nc.Block() as block:

        @block.gpsimd
        def _(pool):
            if first:
                nc.gpsimd.memset(ones8[:, :], 1.0).then_inc(consts, 1)
            else:
                nc.gpsimd.memset(mean_w[:, :], 1.0 / N).then_inc(consts, 1)
            nc.gpsimd.memset(gm[:, H:H + 1], LIFT).then_inc(lifted, 1)
            pool.wait_ge(step, 1)
            nc.gpsimd.partition_all_reduce(g[:, :], gm[:, 0:H], P, RMAX).then_inc(max_ready, 1)

        @block.vector
        def _(dve):
            nc.vector.tensor_reduce(gm[:, 0:H], sc[:, :, S2:S2 + H].rearrange("p t h -> p h t"), AX.X,
                                    ALU.max).then_inc(step, 1)
            nc.vector.tensor_scalar(neg_s2[:, :, :], sc[:, :, S2:S2 + H], -1.0, None, ALU.mult).then_inc(step, 1)
            dve.wait_ge(turned, 1)
            nc.vector.tensor_copy(s_rows[:, :], ps[:, 4, :]).then_inc(step, 1)
            if not first:
                nc.vector.tensor_tensor(mask[:, :, :].bitcast(u16), mask[:, :, :].bitcast(u16),
                                        e_byte[:, :].bitcast(u16).unsqueeze(1).to_broadcast([P, NT, N // 2]),
                                        ALU.bitwise_xor).then_inc(e_ready, 1)
            dve.wait_ge(max_ready, 1)
            gb = g[:, :].unsqueeze(1).to_broadcast([P, NT, H])
            nc.vector.tensor_tensor(sh[:, :, :], sc[:, :, S2:S2 + H], gb, ALU.subtract).then_inc(shifted, 1)
            nc.vector.tensor_tensor(zr[:, :, :], sc[:, :, 0:H], gb, ALU.add).then_inc(step, 1)
            dve.wait_ge(step, 4)
            nc.vector.tensor_scalar(zr[:, :, :], zr[:, :, :], 0.0, None, ALU.max).then_inc(shifted, 1)
            if first:
                dve.wait_ge(degrees, 4)
                nc.vector.tensor_scalar(e_byte[:, :], ps[:, 0:4, :].rearrange("p a b -> p (a b)"), 0.5, float(ONE8),
                                        ALU.is_lt, ALU.mult).then_inc(e_ready, 1)
                nc.vector.tensor_scalar(e_row[:, :], ps[0:1, 0:4, :].rearrange("p a b -> p (a b)"), 0.5, None,
                                        ALU.is_lt).then_inc(e_ready, 1)
                dve.wait_ge(e_ready, 2)
                nc.vector.tensor_tensor(mask[:, :, :].bitcast(u16), mask[:, :, :].bitcast(u16),
                                        e_byte[:, :].bitcast(u16).unsqueeze(1).to_broadcast([P, NT, N // 2]),
                                        ALU.bitwise_or).then_inc(e_ready, 1)
                dve.wait_ge(col_done, 1)
                nc.vector.tensor_copy(e_col[:, :], ps[:, 5, 0:NT]).then_inc(step, 1)
            else:
                dve.wait_ge(degrees, 1)
                nc.vector.tensor_copy(mean[:, :], ps[:, 0, :]).then_inc(step, 1)

        @block.scalar
        def _(act):
            act.wait_ge(shifted, 1)
            act.wait_ge(lifted, 1)
            lift = gm[:, H:H + 1]
            act.activation(bd[:, 0, :, :], sh[:, :, :], ACT.Exp, bias=lift).then_inc(exps, 1)
            act.activation(bd[:, 1, :, :], sh[:, :, :], ACT.Exp, scale=SLOPE).then_inc(exps, 1)
            act.wait_ge(shifted, 2)
            act.activation(ratio[:, :, :], zr[:, :, :], ACT.Exp, scale=SLOPE - 1.0, bias=lift).then_inc(exps, 1)

        @block.tensor
        def _(pe):
            per = P // SC
            for gq in range(NT // per):
                last = nc.tensor.transpose(ps[:, 4, rows(gq)],
                                           sc[:, per * gq:per * gq + per, :].rearrange("p t c -> p (t c)"),
                                           ident[:, :])
            last.then_inc(turned, 1)
            pe.wait_ge(consts, 1)
            if first:
                for c in range(4):
                    for jt in range(NT):
                        last = nc.tensor.matmul(ps[:, c, :], ones8[:, :], mask[:, jt, rows(c, F)].bitcast(fp8),
                                                start=(jt == 0), stop=(jt == NT - 1))
                    last.then_inc(degrees, 1)
                pe.wait_ge(e_ready, 2)
                for it in range(NT):
                    last = nc.tensor.matmul(ps[:, 5, it:it + 1], e_row[0:1, rows(it)], ident[0:1, 0:1],
                                            start=True, stop=True)
                last.then_inc(col_done, 1)
            else:
                for jt in range(NT):
                    last = nc.tensor.matmul(ps[:, 0, :], mean_w[:, :],
                                            v[:, jt, :].rearrange("p (h d) -> p h d", d=D1)[:, :, 0:D],
                                            start=(jt == 0), stop=(jt == NT - 1))
                last.then_inc(degrees, 1)

        @block.sync
        def _(sp):
            sp.wait_ge(step, 3)
            per = P // SC
            view = rows_dram.rearrange("c (g l p) -> l c g p", l=per, p=P)
            for t in range(per):
                sp.dma_start(view[t], s_rows[SC * t:SC * t + H, :].rearrange("c (g p) -> c g p", p=P)
                             ).then_inc(stored, 16)
            sp.wait_ge(stored, 16 * per)


def output_layer(nc, tag, x, x_dram, x2_dram, w, w_dram, bias, bias_dram, v, vt, aT, z, e, ident, ps, sem):
    x_loaded = [sem(f"{tag}_x_loaded{c}") for c in range(4)]
    w_loaded = sem(tag + "_w_loaded")
    staged = sem(tag + "_staged")
    turned = sem(tag + "_turned")
    aT_ready = sem(tag + "_aT_ready")
    summed = sem(tag + "_summed")
    z_ready = sem(tag + "_z_ready")
    low_ready = sem(tag + "_low_ready")
    e_ready = sem(tag + "_e_ready")
    elu_step = sem(tag + "_elu_step")
    x_ready = sem(tag + "_x_ready")
    x_stored = sem(tag + "_x_stored")

    with nc.Block() as block:

        @block.sync
        def _(sp):
            for c in range(4):
                sp.dma_start(x[:, 4 * c:4 * c + 4, :],
                             x_dram[c * 512:(c + 1) * 512, :].rearrange("(t p) f -> p t f", p=P)
                             ).then_inc(x_loaded[c], 16)
            for c in range(4):
                sp.wait_ge(x_ready, 4 * c + 4)
                sp.dma_start(x2_dram[c * 512:(c + 1) * 512, :].rearrange("(t p) f -> p t f", p=P),
                             x[:, 4 * c:4 * c + 4, :]).then_inc(x_stored, 16)
            sp.wait_ge(x_stored, 64)

        @block.gpsimd
        def _(pool):
            def stage(it, b):
                wait_from(pool, turned, it - 1)
                src = (v[:, it, 0:F] if isinstance(it, int) else
                       v[:, bass.ds(it, 1), 0:F].rearrange("p a f -> p (a f)"))
                nc.gpsimd.tensor_copy(vt[:, b, :], src).then_inc(staged, 1)
            tile_pairs(pool, stage)

        @block.scalar
        def _(act):
            act.dma_start(w[:, :, :], w_dram).then_inc(w_loaded, 16)
            act.dma_start(bias[:, :], bias_dram.partition_broadcast(P)).then_inc(w_loaded, 16)

            def low(it, b):
                act.wait_ge(low_ready, it + 1)
                act.activation(e[:, b, :], e[:, b, :], ACT.Exp).then_inc(e_ready, 1)

            def tile(it, b):
                act.wait_ge(turned, it + 1)
                wait_from(act, summed, it - 1)
                act.activation(aT[:, b, :, :], ps[:, b, :].rearrange("p (k i) -> p k i", i=P),
                               ACT.Copy).then_inc(aT_ready, 1)
                if not isinstance(it, int) or it > 0:
                    low(it - 1, 1 - b)
            tile_pairs(act, tile)
            low(NT - 1, 1)

        @block.vector
        def _(dve):
            dve.wait_ge(w_loaded, 32)
            for c in range(4):
                dve.wait_ge(x_loaded[c], 16)

            def finish(it, b):
                dve.wait_ge(e_ready, it + 1)
                nc.vector.scalar_tensor_tensor(z[:, b, :], z[:, b, :], 0.0, e[:, b, :], ALU.max,
                                               ALU.add).then_inc(elu_step, 1)
                dve.wait_ge(elu_step, it + 1)
                dst = x[:, it, :] if isinstance(it, int) else x[:, bass.ds(it, 1), :].rearrange("p a f -> p (a f)")
                nc.vector.scalar_tensor_tensor(dst, z[:, b, :], -1.0, dst, ALU.add, ALU.add).then_inc(x_ready, 1)

            def tile(it, b):
                dve.wait_ge(summed, it + 1)
                wait_from(dve, x_ready, it - 1)
                nc.vector.tensor_tensor(z[:, b, :], ps[:, 2 + b, :], bias[:, :], ALU.add).then_inc(z_ready, 1)
                dve.wait_ge(z_ready, it + 1)
                nc.vector.tensor_scalar(e[:, b, :], z[:, b, :], 0.0, None, ALU.min).then_inc(low_ready, 1)
                if not isinstance(it, int) or it > 0:
                    finish(it - 1, 1 - b)
            tile_pairs(dve, tile)
            finish(NT - 1, 1)

        @block.tensor
        def _(pe):
            def turn(it, b):
                pe.wait_ge(staged, it + 1)
                wait_from(pe, aT_ready, it - 1)
                for k in range(KT):
                    last = nc.tensor.transpose(ps[:, b, rows(k)], vt[:, b, rows(k)], ident[:, :])
                last.then_inc(turned, 1)

            def times_w(it, b):
                pe.wait_ge(aT_ready, it + 1)
                wait_from(pe, z_ready, it - 1)
                for k in range(KT):
                    last = nc.tensor.matmul(ps[:, 2 + b, :], aT[:, b, k, :], w[:, k, :],
                                            start=(k == 0), stop=(k == KT - 1))
                last.then_inc(summed, 1)

            def tile(it, b):
                turn(it, b)
                if isinstance(it, int) and it == 0:
                    pe.wait_ge(w_loaded, 32)
                if not isinstance(it, int) or it > 0:
                    times_w(it - 1, 1 - b)
            tile_pairs(pe, tile)
            times_w(NT - 1, 1)


def mlp(nc, tag, x, x2_dram, out, w_drams, b_drams, raw, wT, b_rows, b_col, b4, v, mean, e_col, z, e, encT, o1, o2, o3,
        ident, ps, sem):
    CT = 4
    w1, w2, w3, w4 = w_drams
    x_loaded = [sem(f"{tag}_x_loaded{c}") for c in range(4)]
    raw_loaded = sem(tag + "_raw_loaded")
    b_loaded = sem(tag + "_b_loaded")
    w_turned = sem(tag + "_w_turned")
    w_ready = sem(tag + "_w_ready")
    z_ready = sem(tag + "_z_ready")
    low_ready = sem(tag + "_low_ready")
    e_ready = sem(tag + "_e_ready")
    enc_ready = sem(tag + "_enc_ready")
    turned = sem(tag + "_turned")
    encT_ready = sem(tag + "_encT_ready")
    l1 = sem(tag + "_l1")
    r1 = sem(tag + "_r1")
    l2 = sem(tag + "_l2")
    r2 = sem(tag + "_r2")
    l3 = sem(tag + "_l3")
    r3 = sem(tag + "_r3")
    l4 = sem(tag + "_l4")
    xb_ready = sem(tag + "_xb_ready")
    y_ready = sem(tag + "_y_ready")
    stored = sem(tag + "_stored")
    W1, W2, W3, W4 = 0, 1024, 1280, 1536

    with nc.Block() as block:

        @block.sync
        def _(sp):
            sp.dma_start(raw[:, 0:1024].rearrange("p (o k) -> p o k", k=512),
                         w1.rearrange("(o p) k -> p o k", p=P)).then_inc(raw_loaded, 16)
            sp.dma_start(raw[:, 1024:1280], w2).then_inc(raw_loaded, 16)
            sp.dma_start(raw[:, 1280:1536].rearrange("p (o k) -> p o k", k=128),
                         w3.rearrange("(o p) k -> p o k", p=P)).then_inc(raw_loaded, 16)
            sp.dma_start(raw[:, 1536:2560].rearrange("p (o k) -> p o k", k=256),
                         w4.rearrange("(o p) k -> p o k", p=P)).then_inc(raw_loaded, 16)
            for c in range(4):
                sp.dma_start(x[:, 4 * c:4 * c + 4, :],
                             x2_dram[c * 512:(c + 1) * 512, :].rearrange("(t p) f -> p t f", p=P)
                             ).then_inc(x_loaded[c], 16)
            for c in range(4):
                sp.wait_ge(y_ready, CT * (c + 1))
                sp.dma_start(out[c * 512:(c + 1) * 512, :].rearrange("(t p) f -> p t f", p=P),
                             x[:, 4 * c:4 * c + 4, :]).then_inc(stored, 16)
            sp.wait_ge(stored, 64)

        @block.scalar
        def _(act):
            act.dma_start(b_rows[0:2, :], b_drams[0].rearrange("(o p) -> o p", p=P)).then_inc(b_loaded, 16)
            act.dma_start(b_rows[2:3, :], b_drams[1].rearrange("(o p) -> o p", p=P)).then_inc(b_loaded, 16)
            act.dma_start(b_rows[3:5, :], b_drams[2].rearrange("(o p) -> o p", p=P)).then_inc(b_loaded, 16)
            act.dma_start(b4[:, :], b_drams[3].partition_broadcast(P)).then_inc(b_loaded, 16)

            def enc_tile(it):
                b = it % 2
                act.wait_ge(low_ready, it + 1)
                act.activation(e[:, b, :], e[:, b, :], ACT.Exp).then_inc(e_ready, 1)
                if it:
                    enc_copy(it - 1)

            def enc_copy(it):
                b = it % 2
                act.wait_ge(turned, it + 1)
                if it >= 8 and it % CT == 0:
                    act.wait_ge(l1, 2 * (it // CT - 1))
                act.activation(encT[:, it // CT % 2, :, rows(it % CT)], ps[:, b, :].rearrange("p (k i) -> p k i", i=P),
                               ACT.Copy, bias=-1.0).then_inc(encT_ready, 1)

            for it in range(CT):
                enc_tile(it)
            act.wait_ge(w_ready, 6)
            for c in range(4):
                more = list(range(CT * (c + 1), CT * (c + 2))) if c < 3 else []
                if not more:
                    enc_copy(NT - 1)
                if more:
                    enc_tile(more[0])
                for o in range(2):
                    act.wait_ge(l1, 2 * c + o + 1)
                    act.activation(o1[:, o, :], ps[:, 2 + o, :], ACT.Relu, bias=b_col[:, o:o + 1]).then_inc(r1, 1)
                if more:
                    enc_tile(more[1])
                act.wait_ge(l2, c + 1)
                act.activation(o2[:, :], ps[:, 4, :], ACT.Relu, bias=b_col[:, 2:3]).then_inc(r2, 1)
                if more:
                    enc_tile(more[2])
                if c:
                    act.wait_ge(l4, CT * c)
                for o in range(2):
                    act.wait_ge(l3, 2 * c + o + 1)
                    act.activation(o3[:, o, :], ps[:, 5 + o, :], ACT.Relu, bias=b_col[:, 3 + o:4 + o]).then_inc(r3, 1)
                if more:
                    enc_tile(more[3])

        @block.vector
        def _(dve):
            def enc_tile(it):
                b = it % 2
                if it >= 2:
                    dve.wait_ge(turned, it - 1)
                nc.vector.scalar_tensor_tensor(z[:, b, :], mean[:, :], e_col[:, it:it + 1], v[:, it, 0:F], ALU.mult,
                                               ALU.add).then_inc(z_ready, 1)
                dve.wait_ge(z_ready, it + 1)
                nc.vector.tensor_scalar(e[:, b, :], z[:, b, :], 0.0, None, ALU.min).then_inc(low_ready, 1)
                if it:
                    enc_end(it - 1)

            def enc_end(it):
                b = it % 2
                dve.wait_ge(e_ready, it + 1)
                nc.vector.scalar_tensor_tensor(z[:, b, :], z[:, b, :], 0.0, e[:, b, :], ALU.max,
                                               ALU.add).then_inc(enc_ready, 1)

            def add_x(c):
                dve.wait_ge(x_loaded[c], 16)
                nc.vector.tensor_tensor(x[:, CT * c:CT * c + CT, :], x[:, CT * c:CT * c + CT, :],
                                        b4[:, :].unsqueeze(1).to_broadcast([P, CT, F]), ALU.add).then_inc(xb_ready, 1)

            def result(it):
                dve.wait_ge(l4, it + 1)
                dve.wait_ge(xb_ready, it // CT + 1)
                nc.vector.tensor_tensor(x[:, it, :], ps[:, (7, 4)[it % 2], :], x[:, it, :], ALU.add).then_inc(y_ready, 1)

            for it in range(CT):
                enc_tile(it)
            dve.wait_ge(w_turned, 6)
            for k in range(5):
                nc.vector.tensor_copy(wT[:, rows(k, F)], ps[:, 2 + k, :]).then_inc(w_ready, 1)
            nc.vector.tensor_copy(b_col[:, :], ps[:, 7, 0:5]).then_inc(w_ready, 1)
            dve.wait_ge(b_loaded, 64)
            for c in range(4):
                if c < 3:
                    for it in range(CT * (c + 1), CT * (c + 2)):
                        enc_tile(it)
                        if c and it % CT == 0:
                            pass
                else:
                    enc_end(NT - 1)
                add_x(c)
                for it in range(CT * c, CT * c + CT):
                    result(it)

        @block.tensor
        def _(pe):
            def turn(it):
                b = it % 2
                pe.wait_ge(enc_ready, it + 1)
                if it >= 2:
                    pe.wait_ge(encT_ready, it - 1)
                for k in range(KT):
                    last = nc.tensor.transpose(ps[:, b, rows(k)], z[:, b, rows(k)], ident[:, :])
                last.then_inc(turned, 1)

            pe.wait_ge(raw_loaded, 64)
            blocks = ([(W1 + 256 * k + P * o, 512 * o + P * k) for k in range(4) for o in range(2)]
                      + [(W2 + P * k, 1024 + P * k) for k in range(2)]
                      + [(W3 + P * o, 1280 + P * o) for o in range(2)]
                      + [(W4 + 512 * k + P * o, 1536 + 256 * o + P * k) for k in range(2) for o in range(4)])
            for n, (to, at) in enumerate(blocks):
                last = nc.tensor.transpose(ps[:, 2 + to // F, to % F:to % F + P], raw[:, at:at + P], ident[:, :])
                if n % 4 == 3:
                    last.then_inc(w_turned, 1)
            pe.wait_ge(b_loaded, 64)
            nc.tensor.transpose(ps[:, 7, 0:5], b_rows[:, :], ident[0:5, 0:5]).then_inc(w_turned, 1)
            for it in range(CT):
                turn(it)
            pe.wait_ge(w_ready, 6)
            for c in range(4):
                more = list(range(CT * (c + 1), CT * (c + 2))) if c < 3 else []
                pe.wait_ge(encT_ready, CT * (c + 1))
                for o in range(2):
                    if c:
                        pe.wait_ge(r1, 2 * c - 1 + o)
                    for k in range(KT):
                        last = nc.tensor.matmul(ps[:, 2 + o, :], wT[:, W1 + 256 * k + P * o:W1 + 256 * k + P * o + P],
                                                encT[:, c % 2, k, :], start=(k == 0), stop=(k == KT - 1))
                    last.then_inc(l1, 1)
                if more:
                    turn(more[0])
                pe.wait_ge(r1, 2 * c + 2)
                if c:
                    pe.wait_ge(y_ready, CT * c)
                for k in range(2):
                    last = nc.tensor.matmul(ps[:, 4, :], wT[:, W2 + P * k:W2 + P * k + P], o1[:, k, :],
                                            start=(k == 0), stop=(k == 1))
                last.then_inc(l2, 1)
                if more:
                    turn(more[1])
                pe.wait_ge(r2, c + 1)
                for o in range(2):
                    nc.tensor.matmul(ps[:, 5 + o, :], wT[:, W3 + P * o:W3 + P * o + P], o2[:, :],
                                     start=True, stop=True).then_inc(l3, 1)
                if more:
                    turn(more[2])
                pe.wait_ge(r3, 2 * c + 2)
                for it in range(CT * c, CT * c + CT):
                    if it >= 2:
                        pe.wait_ge(y_ready, it - 1)
                    for k in range(2):
                        last = nc.tensor.matmul(ps[:, (7, 4)[it % 2], :], o3[:, k, rows(it % CT)],
                                                wT[:, W4 + 512 * k:W4 + 512 * k + 512], start=(k == 0), stop=(k == 1))
                    last.then_inc(l4, 1)
                if more:
                    turn(more[3])


def build(nc, x, adj, w_seq, a1_0, a2_0, w_out, b_out, w_1, a1_1, a2_1, w1, b1, w2, b2, w3, b3, w4, b4, out):
    with ExitStack() as ctx:
        def sem(name):
            return ctx.enter_context(nc.semaphore(name))

        keep = lambda name, shape, dt: ctx.enter_context(nc.sbuf_tensor(name, shape, dt))
        rows_dram = [nc.dram_tensor(f"s1_rows{n}", [h, N], fp32, kind="Internal").ap() for n, h in enumerate((16, 8))]
        x2_dram = nc.dram_tensor("x2", [N, F], fp32, kind="Internal").ap()
        ps = ctx.enter_context(nc.psum_tensor("ps", [P, 8, 512], fp32))
        mask = keep("mask", [P, NT, N], u8)
        v = keep("v", [P, NT, 16 * 33], fp32)
        ident = keep("ident", [P, P], fp32)
        e_col = keep("e_col", [P, NT], fp32)
        mean = keep("mean", [P, F], fp32)
        e_byte = mean[:, :].bitcast(u8)
        for n in range(2):
            H, D = ((16, 32), (8, 64))[n]
            HA = (1, 8)[n]
            D1 = D + 1
            vv = v[:, :, 0:H * D1]
            tag = f"g{n}"
            with ExitStack() as layer:
                own = lambda name, shape, dt, s=layer: s.enter_context(nc.sbuf_tensor(f"{tag}_{name}", shape, dt))
                bd = own("bd", [P, 2, NT, H], fp32)
                ratio = own("ratio", [P, NT, H], fp32)
                neg_s2 = own("neg_s2", [P, NT, H], fp32)
                with ExitStack() as part:
                    tmp_own = lambda name, shape, dt, s=part: s.enter_context(nc.sbuf_tensor(f"{tag}_{name}", shape, dt))
                    xx = tmp_own("x", [P, NT, F], fp32)
                    sc = tmp_own("sc", [P, NT, SC], fp32)
                    adj_t = tmp_own("adj", [P, 2, N], fp32) if n == 0 else None
                    w = tmp_own("w", [P, KT, F], fp32)
                    a_bc = tmp_own("a_bc", [P, 2, HA * D], fp32)
                    wa = tmp_own("wa", [P, KT, SC], fp32)
                    tmp = tmp_own("tmp", [P, 2, F], fp32)
                    xn = tmp_own("xn", [P, 2, F], fp32)
                    hT = tmp_own("hT", [P, 2, KT, P], fp32)
                    stats = tmp_own("stats", [P, NT, 6], fp32)
                    mv = tmp_own("mv", [P, NT, 3], fp32)
                    sh = tmp_own("sh", [P, NT, H], fp32)
                    zr = tmp_own("zr", [P, NT, H], fp32)
                    gm = tmp_own("gm", [P, H + 1], fp32)
                    g = tmp_own("g", [P, H], fp32)
                    s_rows = tmp_own("s_rows", [P, F], fp32)
                    ones8 = tmp_own("ones8", [P, P], bf16)
                    e_row = tmp_own("e_row", [1, N], fp32)
                    mean_w = tmp_own("mean_w", [P, P], fp32)
                    if n == 1:
                        out_w = tmp_own("out_w", [P, KT, F], fp32)
                        out_b = tmp_own("out_b", [P, F], fp32)
                        z = tmp_own("z", [P, 2, F], fp32)
                        e = tmp_own("e", [P, 2, F], fp32)
                        output_layer(nc, "out", xx, x, x2_dram, out_w, w_out.rearrange("(k p) n -> p k n", p=P),
                                     out_b, b_out, v, xn, hT, z, e, ident, ps, sem)
                        w_dram = [w_1[:, rows(kt), :].rearrange("h p d -> p h d") for kt in range(KT)]
                    else:
                        w_dram = [w_seq[rows(kt), :].rearrange("p (h d) -> p h d", d=D) for kt in range(KT)]
                    transform(nc, f"t{n}", H, D, HA, xx, x if n == 0 else None, w_dram,
                              (a1_0, a2_0) if n == 0 else (a1_1.rearrange("h d -> (h d)"), a2_1.rearrange("h d -> (h d)")),
                              vv, w, a_bc, wa, tmp, xn, hT, stats, mv, sc, ident, ps, sem,
                              mask=mask if n == 0 else None, adj=adj_t, adj_dram=adj)
                    factors(nc, f"f{n}", H, D, sc, vv, sh, zr, gm, g, bd, ratio, neg_s2, s_rows, rows_dram[n], mask,
                            ones8, e_row, e_byte, e_col, mean_w, mean if n == 1 else None, ident, ps, sem, n == 0)
                with ExitStack() as part:
                    tmp_own = lambda name, shape, dt, s=part: s.enter_context(nc.sbuf_tensor(f"{tag}_{name}", shape, dt))
                    t_buf = tmp_own("t_buf", [P, 2, NT, HALF], u8)
                    u_buf = tmp_own("u_buf", [P, 2, NT, HALF], u8)
                    s1 = tmp_own("s1", [P, 2, N], fp32)
                    parts = tmp_own("parts", [P, 2, 2, NT, D1, 3], fp32)
                    shift = tmp_own("shift", [P, 2, 2, NT], fp32)
                    sums = tmp_own("sums", [P, NT, 2 * D1] if n == 0 else [P, NT, 2 * D1], fp32)
                    attention(nc, f"a{n}", H, D, (7, 15) if n == 0 else (15,), mask, vv, bd, ratio, neg_s2,
                              rows_dram[n], t_buf, u_buf, s1, parts, shift, sums, ps, sem,
                              empty=e_col if n == 1 else None)
        with ExitStack() as part:
            own = lambda name, shape, dt: part.enter_context(nc.sbuf_tensor("m_" + name, shape, dt))
            mlp(nc, "m", own("x", [P, NT, F], fp32), x2_dram, out, (w1, w2, w3, w4), (b1, b2, b3, b4),
                own("raw", [P, 2560], fp32), own("wT", [P, 2560], fp32), own("b_rows", [5, P], fp32), own("b_col", [P, 5], fp32),
                own("b4", [P, F], fp32), vv, mean, e_col, own("z", [P, 2, F], fp32), own("e", [P, 2, F], fp32),
                own("encT", [P, 2, KT, F], fp32), own("o1", [P, 2, F], fp32), own("o2", [P, F], fp32),
                own("o3", [P, 2, F], fp32), ident, ps, sem)


NAMES = ["x", "adj", "L0_gnn_W_seq", "L0_gnn_a1", "L0_gnn_a2", "L0_gnn_W_out", "L0_gnn_b_out", "L1_gnn_W",
         "L1_gnn_a1", "L1_gnn_a2", "L1_gnn_W1", "L1_gnn_b1", "L1_gnn_W2", "L1_gnn_b2", "L1_gnn_W3", "L1_gnn_b3",
         "L1_gnn_W4", "L1_gnn_b4"]


def kernel(**inputs):
    import numpy as np
    import concourse.bacc as bacc
    from concourse.bass_utils import run_bass_kernel_spmd

    nc = bacc.Bacc("TRN2", target_bir_lowering=False, num_devices=1)
    arrays, args = {}, []
    for name in NAMES:
        a = np.ascontiguousarray(inputs[name])
        arrays["in_" + name] = a
        args.append(nc.dram_tensor("in_" + name, a.shape, mybir.dt.from_np(a.dtype), kind="ExternalInput").ap())
    out = nc.dram_tensor("out_0", (N, F), fp32, kind="ExternalOutput").ap()
    build(nc, *args, out)
    r = run_bass_kernel_spmd(nc, [arrays], core_ids=[0])
    return r.results[0]["out_0"]
```

```python
import concourse.bass as bass
from concourse import mybir
from contextlib import ExitStack

fp32 = mybir.dt.float32
fp32r = mybir.dt.float32r
bf16 = mybir.dt.bfloat16
fp8 = mybir.dt.float8e4
u8 = mybir.dt.uint8
i8 = mybir.dt.int8
u16 = mybir.dt.uint16
ALU = mybir.AluOpType
ACT = mybir.ActivationFunctionType
AX = mybir.AxisListType
RMAX = bass.bass_isa.ReduceOp.max

P = 128
N = 2048
F = 512
NT = N // P
KT = F // P
HALF = N // 2
CH = 4
NC = NT // CH
ONE8 = 56
S2 = 16
SC = 32
LIFT = 60.0
SLOPE = 0.2
EPS = 1e-5


def rows(it, n=P):
    return slice(it * n, (it + 1) * n) if isinstance(it, int) else bass.ds(it * n, n)


def wait_from(eng, sem, value):
    if not isinstance(value, int) or value > 0:
        eng.wait_ge(sem, value)


def pipeline(eng, step, end, first, last, unroll):
    for s in range(first):
        step(s, s)
    with eng.Fori(0, (last - first) // unroll) as m:
        for k in range(first, first + unroll):
            step(unroll * m + k, k)
    for s in range(last, end):
        step(s, s)


def has_tile(t):
    return not isinstance(t, int) or 0 <= t < NT


def tile_of(ap, t):
    return ap[:, t, :] if isinstance(t, int) else ap[:, bass.ds(t, 1), :].rearrange("p a f -> p (a f)")


def split_matmul(nc, out, left, right):
    n = len(left)
    for k in range(n):
        (lh, ll), (rh, rl) = left[k], right[k]
        nc.tensor.matmul(out, lh, rh, start=(k == 0), stop=False)
        nc.tensor.matmul(out, lh, rl, start=False, stop=False)
        last = nc.tensor.matmul(out, ll, rh, start=False, stop=(k == n - 1))
    return last


def score_matmul(nc, out, left, wa_parts):
    n = len(left)
    for k in range(n):
        high = (out[:, 0:2 * SC], left[k][0], wa_parts[:, k, :, :].rearrange("p a c -> p (a c)"))
        low = (out[:, 0:SC], left[k][1], wa_parts[:, k, 0, :])
        for at, stationary, moving in ((high, low) if k < n - 1 else (low, high)):
            last = nc.tensor.matmul(at, stationary, moving, start=(k == 0 and at is high[0]),
                                    stop=(k == n - 1 and at is high[0]))
    return last


def take_scores(nc, to, sums):
    return nc.vector.tensor_reduce(to, sums[:, 0:2 * SC].rearrange("p (a c) -> p c a", a=2), AX.X, ALU.add)


def attention(nc, tag, H, D, dve_tiles, mask, v, sc, small, s_rows, s1_rows, t_buf, u_buf, s1,
              parts, sums, ident, ps, sem, e_col=None, mean=None, mean_w=None, prefetch=()):
    D1 = D + 1
    W3 = 3 * D1
    PAIRS = H // 2
    bd, ratio, neg_s2, sh, zr, gm, g, shift, one_minus_e = small
    act_tiles = [jt for jt in range(NT) if jt not in dve_tiles]
    NA, ND = len(act_tiles), len(dve_tiles)
    STEPS = 4 if mean is None else 3

    s1_loaded = [sem(f"{tag}_s1_loaded{b}") for b in range(2)]
    act_shift = sem(tag + "_act_shift")
    dve_shift = sem(tag + "_dve_shift")
    group_begun = sem(tag + "_group_begun")
    act_compared = sem(tag + "_act_compared")
    dve_compared = sem(tag + "_dve_compared")
    t_ready = sem(tag + "_t_ready")
    u_ready = sem(tag + "_u_ready")
    weighted = sem(tag + "_weighted")
    parts_ready = sem(tag + "_parts_ready")
    group_done = sem(tag + "_group_done")
    group_free = sem(tag + "_group_free")
    post = sem(tag + "_post")

    maxima = sem(tag + "_maxima")
    max_ready = sem(tag + "_max_ready")
    lifted = sem(tag + "_lifted")
    neg_ready = sem(tag + "_neg_ready")
    shifted = sem(tag + "_shifted")
    exps = sem(tag + "_exps")
    sc_turned = sem(tag + "_sc_turned")
    s_rows_ready = sem(tag + "_s_rows_ready")
    rows_stored = sem(tag + "_rows_stored")
    if mean is not None:
        z_ready = sem(tag + "_z_ready")
        exp_ready = sem(tag + "_exp_ready")
        elu_ready = sem(tag + "_elu_ready")
        mean_w_set = sem(tag + "_mean_w_set")
        mean_summed = sem(tag + "_mean_summed")
        mean_ready = sem(tag + "_mean_ready")
        cleared = sem(tag + "_cleared")
    if prefetch:
        prefetched = sem(tag + "_prefetched")

    with nc.Block() as block:

        @block.sync
        def _(sp):
            def load(h, b):
                sp.dma_start(s1[:, b, :], s1_rows[h:h + 1, :].rearrange("a n -> (a n)").partition_broadcast(P)
                             if isinstance(h, int) else
                             s1_rows[bass.ds(h, 1), :].rearrange("a n -> (a n)").partition_broadcast(P)
                             ).then_inc(s1_loaded[b], 16)

            per = P // SC
            view = s1_rows.rearrange("c (g l p) -> l c g p", l=per, p=P)
            sp.wait_ge(s_rows_ready, 1)
            for t in range(per):
                sp.dma_start(view[t], s_rows[SC * t:SC * t + H, :].rearrange("c (g p) -> c g p", p=P)
                             ).then_inc(rows_stored, 16)
            sp.wait_ge(rows_stored, 16 * per)
            load(0, 0)
            load(1, 1)
            for dst, src in prefetch:
                sp.dma_start(dst, src).then_inc(prefetched, 16)
            with sp.Fori(0, PAIRS - 1) as m:
                for b in range(2):
                    sp.wait_ge(t_ready, 4 * NC * m + 2 * NC * (b + 1))
                    load(2 * m + 2 + b, b)
            if prefetch:
                sp.wait_ge(prefetched, 16 * len(prefetch))

        @block.gpsimd
        def _(pool):
            nc.gpsimd.memset(gm[:, H:H + 1], LIFT).then_inc(lifted, 1)
            if mean is not None:
                nc.gpsimd.memset(mean_w, 1.0 / N).then_inc(mean_w_set, 1)
            pool.wait_ge(maxima, 1)
            nc.gpsimd.partition_all_reduce(g[:, :], gm[:, 0:H], P, RMAX).then_inc(max_ready, 1)

        @block.scalar
        def _(act):
            act.wait_ge(sc_turned, 1)
            act.activation(s_rows[:, :], ps[:, 0, :], ACT.Copy).then_inc(s_rows_ready, 1)
            act.wait_ge(shifted, 1)
            act.wait_ge(lifted, 1)
            lift = gm[:, H:H + 1]
            act.activation(bd[:, 0, :, :], sh[:, :, :], ACT.Exp, bias=lift).then_inc(exps, 1)
            act.activation(bd[:, 1, :, :], sh[:, :, :], ACT.Exp, scale=SLOPE).then_inc(exps, 1)
            act.wait_ge(shifted, 3)
            act.activation(ratio[:, :, :], zr[:, :, :], ACT.Exp, scale=SLOPE - 1.0, bias=lift).then_inc(exps, 1)
            act.wait_ge(neg_ready, 1)
            def exp_output(h):
                act.wait_ge(z_ready, 3 * h + 3)
                act.activation(sums[:, :, D1 + 1:2 * D1], sums[:, :, 0:D], ACT.Exp).then_inc(exp_ready, 1)

            def unit(m, k, first=False):
                b, half = k // 2, k % 2
                if half == 0:
                    h = 2 * m + b
                    hs = slice(h, h + 1) if isinstance(m, int) else bass.ds(h, 1)
                    act.activation(shift[:, 0, b, :].unsqueeze(2), neg_s2[:, :, hs], ACT.Copy).then_inc(act_shift, 1)
                    act.wait_ge(act_shift, 2 * m + b + 1)
                    act.wait_ge(s1_loaded[b], 16 * m + 16)
                act.wait_ge(group_done, 8 * m + 2 * k + 2)
                for jt in act_tiles:
                    act.activation(t_buf[:, half, jt, :].bitcast(i8), s1[:, b, half * HALF:(half + 1) * HALF],
                                   ACT.Sign, bias=shift[:, 0, b, jt:jt + 1], scale=-1.0).then_inc(act_compared, 1)
                    if mean is not None and half == 1 and jt == 5 and (b or not first):
                        exp_output(2 * m + b - 1)

            if mean is None:
                with act.Fori(0, PAIRS) as m:
                    for k in range(4):
                        unit(m, k)
            else:
                for k in range(4):
                    unit(0, k, first=True)
                with act.Fori(0, PAIRS - 1) as m:
                    for k in range(4):
                        unit(m + 1, k)
                exp_output(H - 1)

        @block.vector
        def _(dve):
            def split_values(m, b):
                h = 2 * m + b
                w = parts[:, b, :, :, :, :]
                src = v[:, :, h * D1:(h + 1) * D1] if isinstance(m, int) else v[:, :, bass.ds(h * D1, D1)]
                for x in range(2):
                    f = bd[:, x, :, h:h + 1] if isinstance(m, int) else bd[:, x, :, bass.ds(h, 1)]
                    nc.vector.tensor_tensor(w[:, x, :, :, 0], src,
                                            f.to_broadcast([P, NT, D1]), ALU.mult).then_inc(weighted, 1)
                for c in range(1, 3):
                    for x in range(2):
                        dve.wait_ge(weighted, 6 * h + 2 * (c - 1) + x + 1)
                        whole = w[:, x, :, :, c - 1]
                        nc.vector.tensor_tensor(
                            w[:, x, :, :, c], whole,
                            w[:, x, :, :, :].bitcast(bf16)[:, :, :, 2 * c - 1],
                            ALU.subtract).then_inc(weighted, 1)
                dve.wait_ge(weighted, 6 * h + 6)
                dve.sem_inc(parts_ready, 1)

            def take_shift(m, b):
                if not ND:
                    return
                h = 2 * m + b
                hs = slice(h, h + 1) if isinstance(m, int) else bass.ds(h, 1)
                nc.vector.tensor_copy(shift[:, 1, b, :].unsqueeze(2), neg_s2[:, :, hs]).then_inc(dve_shift, 1)
                dve.wait_ge(dve_shift, h + 1)

            def compare(m, k):
                b, half = k // 2, k % 2
                if not ND:
                    return
                if half == 0:
                    dve.wait_ge(s1_loaded[b], 16 * m + 16)
                dve.wait_ge(group_done, 8 * m + 2 * k + 2)
                for jt in dve_tiles:
                    nc.vector.tensor_scalar(t_buf[:, half, jt, :], s1[:, b, half * HALF:(half + 1) * HALF],
                                            shift[:, 1, b, jt:jt + 1], float(ONE8), ALU.is_gt, ALU.mult).then_inc(dve_compared, 1)

            def masks(m, k, c):
                half = k % 2
                jts = slice(c * CH, (c + 1) * CH)
                words = lambda ap: ap.bitcast(u16)
                t = words(t_buf[:, half, jts, :])
                mk = words(mask[:, jts, half * HALF:(half + 1) * HALF])
                na = sum(jt < (c + 1) * CH for jt in act_tiles)
                nd = sum(jt < (c + 1) * CH for jt in dve_tiles)
                dve.wait_ge(act_compared, (4 * m + k) * NA + na)
                if nd:
                    dve.wait_ge(dve_compared, (4 * m + k) * ND + nd)
                nc.vector.tensor_tensor(t, t, mk, ALU.bitwise_and).then_inc(t_ready, 1)

            def rest(m, k, c):
                half = k % 2
                jts = slice(c * CH, (c + 1) * CH)
                words = lambda ap: ap.bitcast(u16)
                dve.wait_ge(t_ready, (4 * m + k) * NC + c + 1)
                nc.vector.tensor_tensor(words(u_buf[:, half, jts, :]), words(t_buf[:, half, jts, :]),
                                        words(mask[:, jts, half * HALF:(half + 1) * HALF]),
                                        ALU.bitwise_xor).then_inc(u_ready, 1)

            def drain(n, slot4, half, g):
                dve.wait_ge(group_done, n + 5)
                it = half * (NT // 2) + 4 * g
                nc.vector.tensor_reduce(sums[:, it:it + 4, :],
                                        ps[:, 4 * g:4 * g + 4, 0:2 * W3].rearrange("p k (m c) -> p k m c", c=3),
                                        AX.X, ALU.add).then_inc(group_free, 1)

            def normalise(m, b):
                h = 2 * m + b
                hs = slice(h, h + 1) if isinstance(h, int) else bass.ds(h, 1)
                vs = slice(h * D, h * D + D) if isinstance(h, int) else bass.ds(h * D, D)
                dve.wait_ge(group_free, 4 * h + 6)
                nc.vector.tensor_tensor(sums[:, :, D1:2 * D1], sums[:, :, D1:2 * D1],
                                        ratio[:, :, hs].to_broadcast([P, NT, D1]), ALU.mult).then_inc(post, 1)
                dve.wait_ge(post, STEPS * h + 1)
                nc.vector.tensor_tensor(sums[:, :, 0:D1], sums[:, :, 0:D1], sums[:, :, D1:2 * D1],
                                        ALU.add).then_inc(post, 1)
                dve.wait_ge(post, STEPS * h + 2)
                nc.vector.reciprocal(sums[:, :, D1:D1 + 1], sums[:, :, D:D1]).then_inc(post, 1)
                dve.wait_ge(post, STEPS * h + 3)
                if mean is None:
                    nc.vector.tensor_tensor(v[:, :, vs], sums[:, :, 0:D],
                                            sums[:, :, D1:D1 + 1].to_broadcast([P, NT, D]), ALU.mult).then_inc(post, 1)
                    return
                nc.vector.tensor_tensor(sums[:, :, D1:D1 + 1], sums[:, :, D1:D1 + 1],
                                        one_minus_e[:, :].unsqueeze(2), ALU.mult).then_inc(cleared, 1)
                nc.vector.tensor_tensor(sums[:, :, D1 + 1:2 * D1], mean[:, vs].unsqueeze(1).to_broadcast([P, NT, D]),
                                        e_col[:, :].unsqueeze(2).to_broadcast([P, NT, D]), ALU.mult).then_inc(z_ready, 1)
                dve.wait_ge(cleared, h + 1)
                nc.vector.tensor_tensor(sums[:, :, 0:D], sums[:, :, 0:D],
                                        sums[:, :, D1:D1 + 1].to_broadcast([P, NT, D]), ALU.mult).then_inc(z_ready, 1)
                dve.wait_ge(z_ready, 3 * h + 2)
                nc.vector.tensor_tensor(sums[:, :, 0:D], sums[:, :, 0:D], sums[:, :, D1 + 1:2 * D1],
                                        ALU.add).then_inc(z_ready, 1)

            def elu(m, b):
                h = 2 * m + b
                vs = slice(h * D, h * D + D) if isinstance(h, int) else bass.ds(h * D, D)
                dve.wait_ge(exp_ready, h + 1)
                nc.vector.tensor_scalar(sums[:, :, D1 + 1:2 * D1], sums[:, :, D1 + 1:2 * D1], 1.0, -1.0, ALU.min,
                                        ALU.add).then_inc(elu_ready, 1)
                dve.wait_ge(elu_ready, 2 * h + 1)
                nc.vector.tensor_tensor(v[:, :, vs], sums[:, :, 0:D], sums[:, :, D1 + 1:2 * D1],
                                        ALU.max).then_inc(elu_ready, 1)
                dve.wait_ge(elu_ready, 2 * h + 2)

            def unit(m, k, first=False):
                b, half = k // 2, k % 2
                if half == 0:
                    take_shift(m, b)
                    split_values(m, b)
                compare(m, k)
                before = half != 0 or b != 0 or not first
                pk = (k - 1) % 4
                n = 8 * m + 2 * k - 2
                masks(m, k, 0)
                masks(m, k, 1)
                rest(m, k, 0)
                rest(m, k, 1)
                if mean is not None and half == 1 and (b or not first):
                    elu(m if b else m - 1, 1 - b)
                if before:
                    drain(n, None, pk % 2, 0)
                masks(m, k, 2)
                masks(m, k, 3)
                rest(m, k, 2)
                rest(m, k, 3)
                if before:
                    drain(n + 1, None, pk % 2, 1)
                    if half == 0:
                        normalise(m if b else m - 1, 1 - b)

            nc.vector.tensor_reduce(gm[:, 0:H], sc[:, :, S2:S2 + H].rearrange("p t h -> p h t"), AX.X,
                                    ALU.max).then_inc(maxima, 1)
            nc.vector.tensor_scalar(neg_s2[:, :, :], sc[:, :, S2:S2 + H], -1.0, None, ALU.mult).then_inc(neg_ready, 1)
            if e_col is not None:
                nc.vector.tensor_scalar(one_minus_e[:, :], e_col[:, :], -1.0, 1.0, ALU.mult,
                                        ALU.add).then_inc(neg_ready, 1)
            dve.wait_ge(max_ready, 1)
            gb = g[:, :].unsqueeze(1).to_broadcast([P, NT, H])
            nc.vector.tensor_tensor(sh[:, :, :], sc[:, :, S2:S2 + H], gb, ALU.subtract).then_inc(shifted, 1)
            nc.vector.tensor_tensor(zr[:, :, :], sc[:, :, 0:H], gb, ALU.add).then_inc(shifted, 1)
            dve.wait_ge(shifted, 2)
            nc.vector.tensor_scalar(zr[:, :, :], zr[:, :, :], 0.0, None, ALU.max).then_inc(shifted, 1)
            if mean is not None:
                dve.wait_ge(mean_summed, 1)
                nc.vector.tensor_copy(mean[:, :], ps[:, 0, :]).then_inc(mean_ready, 1)
                dve.wait_ge(neg_ready, 2)
                dve.wait_ge(mean_ready, 1)
            dve.wait_ge(exps, 3)
            dve.wait_ge(s_rows_ready, 1)
            dve.sem_inc(group_free, 2)
            for k in range(4):
                unit(0, k, first=True)
            with dve.Fori(0, PAIRS - 1) as m:
                for k in range(4):
                    unit(m + 1, k)
            drain(4 * H - 2, None, 1, 0)
            drain(4 * H - 1, None, 1, 1)
            normalise(PAIRS - 1, 1)
            if mean is not None:
                elu(PAIRS - 1, 1)

        @block.tensor
        def _(pe):
            per = P // SC
            for gq in range(NT // per):
                last = nc.tensor.transpose(ps[:, 0, rows(gq)],
                                           sc[:, per * gq:per * gq + per, :].rearrange("p t c -> p (t c)"),
                                           ident[:, :])
            last.then_inc(sc_turned, 1)
            if mean is not None:
                pe.wait_ge(mean_w_set, 1)
                pe.wait_ge(s_rows_ready, 1)
                for jt in range(NT):
                    last = nc.tensor.matmul(ps[:, 0, :], mean_w,
                                            v[:, jt, :].rearrange("p (h d) -> p h d", d=D1)[:, :, 0:D],
                                            start=(jt == 0), stop=(jt == NT - 1))
                last.then_inc(mean_summed, 1)
            pe.sem_inc(group_done, 4)
            with pe.Fori(0, PAIRS) as m:
                for k in range(4):
                    b, half = k // 2, k % 2
                    if half == 0:
                        pe.wait_ge(parts_ready, 2 * m + b + 1)
                    pe.wait_ge(u_ready, 4 * NC * m + NC * (k + 1))
                    for g in range(2):
                        pe.wait_ge(group_free, 8 * m + 2 * k + g + 1)
                        pe.sem_inc(group_begun, 1)
                        for q in range(4):
                            it = 4 * g + q
                            for x, side in enumerate((t_buf, u_buf)):
                                for jt in range(NT):
                                    last = nc.tensor.matmul(
                                        ps[:, it, x * W3:(x + 1) * W3],
                                        side[:, half, jt, it * P:(it + 1) * P].bitcast(fp8),
                                        parts[:, b, x, jt, :, :].rearrange("p d c -> p (d c)").bitcast(bf16)[:, 1::2],
                                        start=(jt == 0), stop=(jt == NT - 1))
                        last.then_inc(group_done, 1)


def layer_norm_stats(nc, dve, x, b, stats, mv, var_eps, sems, t):
    stats_ready, stats_seen, mean_ready, var_ready = sems
    nc.vector.bn_stats(stats[:, b, :], x).then_inc(stats_ready, 1)
    dve.wait_ge(stats_ready, t + 1)
    dve.sem_inc(stats_seen, 1)
    nc.vector.bn_aggr(mv[:, b, :], stats[:, b, :]).then_inc(mean_ready, 1)
    dve.wait_ge(mean_ready, t + 1)
    nc.vector.tensor_scalar(var_eps[:, b, :], mv[:, b, 1:2], EPS, None, ALU.add).then_inc(var_ready, 1)


def attention_vectors(nc, tag, H, D, HA, w, w_parts, a_bc, prod, wa, wa_parts, sem, loads):
    if loads:
        loaded = sem(tag + "_wa_loaded")
    zeroed = sem(tag + "_wa_zeroed")
    products = sem(tag + "_wa_products")
    product_1 = sem(tag + "_wa_product1")
    wa_ready = sem(tag + "_wa_ready")
    high = sem(tag + "_w_high")
    split = sem(tag + "_w_split")
    PARTS = KT + 2

    def load(eng, w_dram, a_dram):
        for kt in range(KT):
            eng.dma_start(w[:, kt, :].rearrange("p (h d) -> p h d", d=D), w_dram[kt]).then_inc(loaded, 16)
        for a, src in enumerate(a_dram):
            eng.dma_start(a_bc[:, a, :], src.partition_broadcast(P)).then_inc(loaded, 16)

    def product(eng, a, k0, k1):
        vec = a_bc[:, a, :].rearrange("p (h d) -> p h d", d=D)
        n = k1 - k0
        if n == 1:
            vec = vec.to_broadcast([P, H, D]) if HA == 1 else vec
            at, by = prod[:, KT * a + k0, :], w[:, k0, :]
            at, by = (ap.rearrange("p (h d) -> p h d", d=D) for ap in (at, by))
        else:
            vec = vec.unsqueeze(1).to_broadcast([P, n, H, D])
            at, by = prod[:, KT * a + k0:KT * a + k1, :], w[:, k0:k1, :]
            at, by = (ap.rearrange("p k (h d) -> p k h d", d=D) for ap in (at, by))
        return eng.tensor_tensor(at, by, vec, ALU.mult)

    def pool_part(pool):
        nc.gpsimd.memset(wa[:, :, :], 0.0).then_inc(zeroed, 1)
        if loads:
            pool.wait_ge(loaded, 16 * PARTS)
        for k in range(KT):
            product(nc.gpsimd, 0, k, k + 1).then_inc(products, 1)

    def act_part(act):
        if loads:
            act.wait_ge(loaded, 16 * PARTS)
        act.activation(w_parts[0][:, :, :], w[:, :, :], ACT.Copy).then_inc(high, 1)

    def dve_w(dve):
        dve.wait_ge(high, 1)
        nc.vector.tensor_tensor(w_parts[1][:, :, :], w[:, :, :], w_parts[0][:, :, :].bitcast(fp32),
                                ALU.subtract).then_inc(split, 1)

    def dve_wa(dve):
        if loads:
            dve.wait_ge(loaded, 16 * PARTS)
        product(nc.vector, 1, 0, KT).then_inc(product_1, 1)
        dve.wait_ge(zeroed, 1)
        for a in (1, 0):
            dve.wait_ge(*((products, KT), (product_1, 1))[a])
            nc.vector.tensor_reduce(wa[:, :, S2 * a:S2 * a + H],
                                    prod[:, KT * a:KT * a + KT, :].rearrange("p k (h d) -> p k h d", d=D),
                                    AX.X, ALU.add).then_inc(wa_ready, 1)
        dve.wait_ge(wa_ready, 2)
        nc.vector.tensor_copy(wa_parts[:, :, 0, :], wa[:, :, :]).then_inc(split, 1)
        dve.wait_ge(split, 2)
        nc.vector.tensor_tensor(wa_parts[:, :, 1, :], wa[:, :, :], wa_parts[:, :, 0, :].bitcast(fp32),
                                ALU.subtract).then_inc(split, 1)

    return load, pool_part, act_part, dve_w, dve_wa, split


def first_transform(nc, tag, x_dram, adj_dram, w_dram, a_dram, v, mask, e_col, w, w_parts, a_bc, prod, wa, wa_parts,
                    xs, adj, adj_b, ident_b, deg, xn, h_parts, stats, mv, var_eps, half, rstd, sc, ident, ps, sem):
    H, D = 16, 32
    D1 = D + 1
    load_w, pool_w, act_w, dve_w, dve_wa, w_split = attention_vectors(
        nc, tag, H, D, 1, w, w_parts, a_bc, prod, wa, wa_parts, sem, loads=True)
    x_loaded = [sem(f"{tag}_x_loaded{k}") for k in range(4)]
    adj_loaded = [sem(f"{tag}_adj_loaded{k}") for k in range(4)]
    const = sem(tag + "_const")
    ln = [sem(tag + n) for n in ("_stats_ready", "_stats_seen", "_mean_ready", "_var_ready")]
    rstd_ready = sem(tag + "_rstd_ready")
    deg_ready = sem(tag + "_deg_ready")
    e_ready = sem(tag + "_e_ready")
    filled = sem(tag + "_filled")
    xn_ready = sem(tag + "_xn_ready")
    turned = sem(tag + "_turned")
    high_ready = sem(tag + "_high_ready")
    low_ready = sem(tag + "_low_ready")
    v_summed = sem(tag + "_v_summed")
    s_summed = sem(tag + "_s_summed")
    v_out = sem(tag + "_v_out")
    s_out = sem(tag + "_s_out")
    adj_turned = sem(tag + "_adj_turned")
    mask_dve = sem(tag + "_mask_dve")
    mask_act = sem(tag + "_mask_act")
    vh = v.rearrange("p t (h d) -> p t h d", d=D1)

    def run(eng, step):
        pipeline(eng, step, NT + 2, 4, NT, 4)

    with nc.Block() as block:

        @block.sync
        def _(sp):
            def step(s, k):
                if has_tile(s):
                    wait_from(sp, xn_ready, s - 3)
                    sp.dma_start(xs[:, k % 4, :], x_dram[rows(s), :]).then_inc(x_loaded[k % 4], 16)
                    wait_from(sp, deg_ready, s - 3)
                    sp.dma_start(adj[:, k % 4, :], adj_dram[rows(s), :]).then_inc(adj_loaded[k % 4], 16)
                if isinstance(s, int) and s == 0:
                    load_w(sp, w_dram, a_dram)
            run(sp, step)

        @block.gpsimd
        def _(pool):
            nc.gpsimd.memset(half[:, 0:1], -0.5).then_inc(const, 1)
            nc.gpsimd.memset(ident[:, :], 0.0).then_inc(const, 1)
            pool.wait_ge(const, 2)
            nc.gpsimd.affine_select(out=ident[:, :], in_=ident[:, :], compare_op=ALU.not_equal, fill=1.0,
                                    base=0, pattern=[[-1, P]], channel_multiplier=1).then_inc(const, 1)
            pool.wait_ge(const, 3)
            nc.gpsimd.tensor_copy(ident_b[:, :], ident[:, :]).then_inc(const, 1)
            nc.gpsimd.memset(vh[:, :, :, D:D1], 1.0).then_inc(const, 1)

            def step(s, k):
                if has_tile(s):
                    pool.wait_ge(ln[3], s + 1)
                    wait_from(pool, xn_ready, s - 1)
                    nc.gpsimd.tensor_tensor(rstd[:, k % 2, :], var_eps[:, k % 2, :], half[:, 0:1],
                                            ALU.pow).then_inc(rstd_ready, 1)
                if isinstance(s, int) and s == 0:
                    pool_w(pool)
            run(pool, step)

        @block.scalar
        def _(act):
            def copy_mask(t, q):
                act.wait_ge(adj_turned, 2 * t + q + 1)
                act.activation(mask[:, 8 * q:8 * q + 8, rows(t)],
                               ps[:, 7, :].bitcast(bf16).rearrange("p (j i) -> p j i", i=P),
                               ACT.Copy, scale=float(ONE8)).then_inc(mask_act, 1)

            def step(s, k):
                if has_tile(s):
                    act.wait_ge(adj_loaded[k % 4], 4 * (s - k % 4) + 16)
                    wait_from(act, e_ready, s - 1)
                    wait_from(act, adj_turned, 2 * s - 2)
                    act.activation(adj_b[:, k % 2, :], adj[:, k % 4, :], ACT.Copy,
                                   accum_out=deg[:, k % 2, :]).then_inc(deg_ready, 1)
                if has_tile(s - 1):
                    b = (k - 1) % 2
                    act.wait_ge(turned, s)
                    wait_from(act, s_summed, s - 2)
                    act.activation(h_parts[0][:, b, :, :], ps[:, b, :].rearrange("p (k i) -> p k i", i=P),
                                   ACT.Relu).then_inc(high_ready, 1)
                if isinstance(s, int) and s == 1:
                    act_w(act)
                if has_tile(s - 1):
                    copy_mask(s - 1, 1)
                if has_tile(s - 2):
                    act.wait_ge(v_summed, s - 1)
                    t = s - 2
                    dst = vh[:, t, :, 0:D] if isinstance(t, int) else (
                        vh[:, bass.ds(t, 1), :, 0:D].rearrange("p a h d -> p (a h) d"))
                    act.activation(dst, ps[:, 2 + k % 2, :].rearrange("p (h d) -> p h d", d=D),
                                   ACT.Copy).then_inc(v_out, 1)
            run(act, step)

        @block.vector
        def _(dve):
            def copy_mask(t, q):
                dve.wait_ge(adj_turned, 2 * t + q + 1)
                nc.vector.tensor_scalar(mask[:, 8 * q:8 * q + 8, rows(t)],
                                        ps[:, 6, :].bitcast(bf16).rearrange("p (j i) -> p j i", i=P),
                                        float(ONE8), None, ALU.mult).then_inc(mask_dve, 1)

            def step(s, k):
                if has_tile(s):
                    b = k % 2
                    dve.wait_ge(x_loaded[k % 4], 4 * (s - k % 4) + 16)
                    layer_norm_stats(nc, dve, xs[:, k % 4, :], b, stats, mv, var_eps, ln, s)
                if has_tile(s):
                    dve.wait_ge(deg_ready, s + 1)
                    e = e_col[:, s:s + 1] if isinstance(s, int) else e_col[:, bass.ds(s, 1)]
                    nc.vector.tensor_scalar(e, deg[:, b, :], 0.5, None, ALU.is_lt).then_inc(e_ready, 1)
                    dve.wait_ge(e_ready, s + 1)
                    nc.vector.tensor_scalar(adj_b[:, b, :], adj_b[:, b, :], e, None, ALU.add).then_inc(filled, 1)
                    dve.wait_ge(rstd_ready, s + 1)
                    wait_from(dve, turned, s - 1)
                    nc.vector.tensor_scalar(xn[:, b, :], xs[:, k % 4, :], mv[:, b, 0:1], rstd[:, b, :],
                                            ALU.subtract, ALU.mult).then_inc(xn_ready, 1)
                if has_tile(s - 1):
                    b = (k - 1) % 2
                    dve.wait_ge(high_ready, s)
                    nc.vector.scalar_tensor_tensor(
                        h_parts[1][:, b, :, :].rearrange("p k i -> p (k i)"), ps[:, b, :], 0.0,
                        h_parts[0][:, b, :, :].rearrange("p k i -> p (k i)").bitcast(fp32), ALU.max,
                        ALU.subtract).then_inc(low_ready, 1)
                if isinstance(s, int) and s == 1:
                    dve_w(dve)
                    dve_wa(dve)
                if has_tile(s - 1):
                    copy_mask(s - 1, 0)
                if has_tile(s - 2):
                    dve.wait_ge(s_summed, s - 1)
                    take_scores(nc, tile_of(sc, s - 2), ps[:, 4 + k % 2, :]).then_inc(s_out, 1)
            run(dve, step)

        @block.tensor
        def _(pe):
            pe.wait_ge(const, 5)

            def turn_adj(t, k, q):
                if q == 0:
                    pe.wait_ge(filled, t + 1)
                wait_from(pe, (mask_dve, mask_act)[q], t)
                for j in range(8):
                    last = nc.tensor.transpose(ps[:, 6 + q, :].bitcast(bf16)[:, rows(j)],
                                               adj_b[:, k % 2, rows(8 * q + j)], ident_b[:, :])
                last.then_inc(adj_turned, 1)

            def step(s, k):
                if has_tile(s - 1):
                    b = (k - 1) % 2
                    pe.wait_ge(xn_ready, s)
                    wait_from(pe, low_ready, s - 2)
                    for kt in range(KT):
                        last = nc.tensor.transpose(ps[:, b, rows(kt)], xn[:, b, rows(kt)], ident[:, :])
                    last.then_inc(turned, 1)
                    turn_adj(s - 1, k - 1, 0)
                if has_tile(s - 2):
                    b = k % 2
                    if isinstance(s, int) and s == 2:
                        pe.wait_ge(w_split, 3)
                    pe.wait_ge(low_ready, s - 1)
                    wait_from(pe, v_out, s - 3)
                    hs = [(h_parts[0][:, b, kt, :], h_parts[1][:, b, kt, :]) for kt in range(KT)]
                    split_matmul(nc, ps[:, 2 + b, :], hs,
                                 [(w_parts[0][:, kt, :], w_parts[1][:, kt, :]) for kt in range(KT)]
                                 ).then_inc(v_summed, 1)
                    wait_from(pe, s_out, s - 3)
                    score_matmul(nc, ps[:, 4 + b, :], hs, wa_parts).then_inc(s_summed, 1)
                if has_tile(s - 1):
                    turn_adj(s - 1, k - 1, 1)
            run(pe, step)


def middle(nc, tag, x_dram, x2_dram, v, out_w, out_parts, out_b, w, w_parts, a_bc, prod, wa, wa_parts, vt, a_parts,
           z, e, xs, xn, h_parts, stats, mv, var_eps, half, rstd, sc, v2, ident, ps, sem):
    H, D = 8, 64
    D1 = D + 1
    _, pool_w, act_w, dve_w, dve_wa, w_split = attention_vectors(
        nc, tag, H, D, H, w, w_parts, a_bc, prod, wa, wa_parts, sem, loads=False)
    x_loaded = [sem(f"{tag}_x_loaded{k}") for k in range(4)]
    stored = [sem(f"{tag}_stored{k}") for k in range(4)]
    const = sem(tag + "_const")
    ones_set = sem(tag + "_ones_set")
    one_b = sem(tag + "_one_b")
    out_high = sem(tag + "_out_high")
    out_split = sem(tag + "_out_split")
    staged = sem(tag + "_staged")
    a_turned = sem(tag + "_a_turned")
    a_high = sem(tag + "_a_high")
    a_low = sem(tag + "_a_low")
    summed = sem(tag + "_summed")
    z_ready = sem(tag + "_z_ready")
    exp_ready = sem(tag + "_exp_ready")
    elu_ready = sem(tag + "_elu_ready")
    x_ready = sem(tag + "_x_ready")
    ln = [sem(tag + n) for n in ("_stats_ready", "_stats_seen", "_mean_ready", "_var_ready")]
    rstd_ready = sem(tag + "_rstd_ready")
    xn_ready = sem(tag + "_xn_ready")
    turned = sem(tag + "_turned")
    high_ready = sem(tag + "_high_ready")
    low_ready = sem(tag + "_low_ready")
    v_summed = sem(tag + "_v_summed")
    s_summed = sem(tag + "_s_summed")
    v_out = sem(tag + "_v_out")
    s_out = sem(tag + "_s_out")
    vh = v2.rearrange("p t (h d) -> p t h d", d=D1)

    def run(eng, step):
        pipeline(eng, step, NT + 4, 4, NT, 4)

    with nc.Block() as block:

        @block.sync
        def _(sp):
            def step(s, k):
                if has_tile(s):
                    wait_from(sp, xn_ready, s - 3)
                    wait_from(sp, stored[k % 4], 4 * (s - k % 4))
                    sp.dma_start(xs[:, k % 4, :], x_dram[rows(s), :]).then_inc(x_loaded[k % 4], 16)
                if has_tile(s - 1):
                    sp.wait_ge(x_ready, s)
                    sp.dma_start(x2_dram[rows(s - 1), :], xs[:, (k - 1) % 4, :]).then_inc(stored[(k - 1) % 4], 16)
            run(sp, step)
            for k in range(4):
                sp.wait_ge(stored[k], 16 * NT // 4)

        @block.gpsimd
        def _(pool):
            def step(s, k):
                if has_tile(s):
                    wait_from(pool, a_turned, s - 1)
                    nc.gpsimd.tensor_copy(vt[:, k % 2, :], tile_of(v, s)[:, 0:F]).then_inc(staged, 1)
                if isinstance(s, int) and s == 1:
                    pool_w(pool)
                if has_tile(s - 2):
                    pool.wait_ge(ln[3], s - 1)
                    wait_from(pool, xn_ready, s - 3)
                    nc.gpsimd.tensor_tensor(rstd[:, k % 2, :], var_eps[:, k % 2, :], half[:, 0:1],
                                            ALU.pow).then_inc(rstd_ready, 1)
                if isinstance(s, int) and s == NT:
                    pool.wait_ge(staged, NT)
                    nc.gpsimd.memset(vh[:, :, :, D:D1], 1.0).then_inc(ones_set, 1)
            run(pool, step)

        @block.scalar
        def _(act):
            act.activation(out_parts[0][:, :, :], out_w[:, :, :], ACT.Copy).then_inc(out_high, 1)

            def step(s, k):
                if has_tile(s):
                    b = k % 2
                    act.wait_ge(a_turned, s + 1)
                    wait_from(act, summed, s - 1)
                    act.activation(a_parts[0][:, b, :, :], ps[:, 0, :].rearrange("p (k i) -> p k i", i=P),
                                   ACT.Copy).then_inc(a_high, 1)
                if isinstance(s, int) and s == 0:
                    act_w(act)
                if has_tile(s - 3):
                    b = (k - 3) % 2
                    act.wait_ge(turned, s - 2)
                    wait_from(act, s_summed, s - 4)
                    act.activation(h_parts[0][:, b, :, :], ps[:, 1, :].rearrange("p (k i) -> p k i", i=P),
                                   ACT.Relu).then_inc(high_ready, 1)
                if has_tile(s - 1):
                    b = (k - 1) % 2
                    act.wait_ge(z_ready, s)
                    wait_from(act, elu_ready, s - 2)
                    act.activation(e[:, b, :], z[:, b, :], ACT.Exp, bias=minus_one).then_inc(exp_ready, 1)
                if has_tile(s - 4):
                    act.wait_ge(v_summed, s - 3)
                    t = s - 4
                    dst = vh[:, t, :, 0:D] if isinstance(t, int) else (
                        vh[:, bass.ds(t, 1), :, 0:D].rearrange("p a h d -> p (a h) d"))
                    act.activation(dst, ps[:, 4 + k % 2, :].rearrange("p (h d) -> p h d", d=D),
                                   ACT.Copy).then_inc(v_out, 1)
            minus_one = half[:, 1:2]
            act.sem_inc(v_out, 1)
            act.wait_ge(const, 1)
            run(act, step)

        @block.vector
        def _(dve):
            dve.sem_inc(s_out, 1)
            nc.vector.memset(half[:, 1:2], -1.0).then_inc(const, 1)
            nc.vector.tensor_scalar(out_b[:, :], out_b[:, :], 1.0, None, ALU.add).then_inc(one_b, 1)
            dve.wait_ge(out_high, 1)
            nc.vector.tensor_tensor(out_parts[1][:, :, :], out_w[:, :, :], out_parts[0][:, :, :].bitcast(fp32),
                                    ALU.subtract).then_inc(out_split, 1)

            def step(s, k):
                if has_tile(s):
                    b = k % 2
                    dve.wait_ge(a_high, s + 1)
                    nc.vector.tensor_tensor(
                        a_parts[1][:, b, :, :].rearrange("p k i -> p (k i)"), ps[:, 0, :],
                        a_parts[0][:, b, :, :].rearrange("p k i -> p (k i)").bitcast(fp32),
                        ALU.subtract).then_inc(a_low, 1)
                if isinstance(s, int) and s == 1:
                    dve_w(dve)
                if has_tile(s - 2):
                    b = k % 2
                    dve.wait_ge(rstd_ready, s - 1)
                    wait_from(dve, turned, s - 3)
                    nc.vector.tensor_scalar(xn[:, b, :], xs[:, (k - 2) % 4, :], mv[:, b, 0:1], rstd[:, b, :],
                                            ALU.subtract, ALU.mult).then_inc(xn_ready, 1)
                if has_tile(s - 1):
                    b = (k - 1) % 2
                    dve.wait_ge(summed, s)
                    wait_from(dve, x_ready, s - 2)
                    if isinstance(s, int) and s == 1:
                        dve.wait_ge(one_b, 1)
                    nc.vector.tensor_tensor(z[:, b, :], ps[:, 2 + b, :], out_b[:, :], ALU.add).then_inc(z_ready, 1)
                if has_tile(s - 3):
                    b = (k - 3) % 2
                    dve.wait_ge(high_ready, s - 2)
                    nc.vector.scalar_tensor_tensor(
                        h_parts[1][:, b, :, :].rearrange("p k i -> p (k i)"), ps[:, 1, :], 0.0,
                        h_parts[0][:, b, :, :].rearrange("p k i -> p (k i)").bitcast(fp32), ALU.max,
                        ALU.subtract).then_inc(low_ready, 1)
                if has_tile(s - 1):
                    b = (k - 1) % 2
                    xt = xs[:, (k - 1) % 4, :]
                    dve.wait_ge(exp_ready, s)
                    nc.vector.scalar_tensor_tensor(z[:, b, :], e[:, b, :], 1.0, z[:, b, :], ALU.min,
                                                   ALU.max).then_inc(elu_ready, 1)
                    dve.wait_ge(elu_ready, s)
                    dve.wait_ge(x_loaded[(k - 1) % 4], 4 * (s - 1 - (k - 1) % 4) + 16)
                    nc.vector.scalar_tensor_tensor(xt, z[:, b, :], -1.0, xt, ALU.add, ALU.add).then_inc(x_ready, 1)
                    dve.wait_ge(x_ready, s)
                    layer_norm_stats(nc, dve, xt, b, stats, mv, var_eps, ln, s - 1)
                if isinstance(s, int) and s == 1:
                    dve_wa(dve)
                if has_tile(s - 4):
                    dve.wait_ge(s_summed, s - 3)
                    take_scores(nc, tile_of(sc, s - 4), ps[:, 6 + k % 2, :]).then_inc(s_out, 1)
            run(dve, step)

        @block.tensor
        def _(pe):
            def step(s, k):
                if has_tile(s):
                    pe.wait_ge(staged, s + 1)
                    wait_from(pe, a_low, s)
                    for kt in range(KT):
                        last = nc.tensor.transpose(ps[:, 0, rows(kt)], vt[:, k % 2, rows(kt)], ident[:, :])
                    last.then_inc(a_turned, 1)
                if has_tile(s - 1):
                    b = (k - 1) % 2
                    if isinstance(s, int) and s == 1:
                        pe.wait_ge(out_split, 1)
                    pe.wait_ge(a_low, s)
                    wait_from(pe, z_ready, s - 2)
                    split_matmul(nc, ps[:, 2 + b, :],
                                 [(a_parts[0][:, b, kt, :], a_parts[1][:, b, kt, :]) for kt in range(KT)],
                                 [(out_parts[0][:, kt, :], out_parts[1][:, kt, :]) for kt in range(KT)]
                                 ).then_inc(summed, 1)
                if has_tile(s - 3):
                    b = (k - 3) % 2
                    pe.wait_ge(xn_ready, s - 2)
                    wait_from(pe, low_ready, s - 3)
                    for kt in range(KT):
                        last = nc.tensor.transpose(ps[:, 1, rows(kt)], xn[:, b, rows(kt)], ident[:, :])
                    last.then_inc(turned, 1)
                if has_tile(s - 4):
                    b = k % 2
                    if isinstance(s, int) and s == 4:
                        pe.wait_ge(w_split, 3)
                    pe.wait_ge(low_ready, s - 3)
                    wait_from(pe, v_out, s - 4)
                    hs = [(h_parts[0][:, b, kt, :], h_parts[1][:, b, kt, :]) for kt in range(KT)]
                    split_matmul(nc, ps[:, 4 + b, :], hs,
                                 [(w_parts[0][:, kt, :], w_parts[1][:, kt, :]) for kt in range(KT)]
                                 ).then_inc(v_summed, 1)
                    wait_from(pe, s_out, s - 4)
                    score_matmul(nc, ps[:, 6 + b, :], hs, wa_parts).then_inc(s_summed, 1)
            run(pe, step)


def mlp(nc, tag, x, x2_dram, out, w_drams, b_drams, raw, wT, b_rows, b_col, b4, v, enc_parts, o, o_parts, ident,
        ps, sem):
    CT = 4
    w1, w2, w3, w4 = w_drams
    x_loaded = [sem(f"{tag}_x_loaded{c}") for c in range(4)]
    raw_loaded = sem(tag + "_raw_loaded")
    b_loaded = sem(tag + "_b_loaded")
    b_turned = sem(tag + "_b_turned")
    b_ready = sem(tag + "_b_ready")
    w_turned = sem(tag + "_w_turned")
    w_high = sem(tag + "_w_high")
    w_ready = sem(tag + "_w_ready")
    turned = sem(tag + "_turned")
    enc_high = sem(tag + "_enc_high")
    enc_low = sem(tag + "_enc_low")
    layer = [sem(f"{tag}_layer{n}") for n in (1, 2, 3)]
    high = [sem(f"{tag}_high{n}") for n in (1, 2, 3)]
    low = [sem(f"{tag}_low{n}") for n in (1, 2, 3)]
    l4 = sem(tag + "_l4")
    xb_ready = sem(tag + "_xb_ready")
    y_ready = sem(tag + "_y_ready")
    stored = sem(tag + "_stored")
    W1, W2, W3, W4 = 0, 1024, 1280, 1536
    HALVES = (2, 1, 2)
    BANK = ((2, 3), (4,), (6, 5))
    BIAS = (0, 2, 3)
    BANK4 = (5, 7)
    wH, wL = wT

    def w_at(start, n):
        return wH[:, start:start + n], wL[:, start:start + n]

    def schedule(c, enc, hidden, fourth):
        hidden(c, 0)
        for n in range(CT):
            enc(c + 1, n)
            fourth(c - 1, n)
            if n == 1:
                hidden(c, 1)
        hidden(c, 2)

    def run(enc, hidden, fourth):
        chunk = lambda f: lambda c, n: f(c, n) if 0 <= c < NT // CT else None
        for c in range(NT // CT + 1):
            schedule(c, chunk(lambda a, n: enc(CT * a + n)), chunk(hidden), chunk(lambda a, n: fourth(CT * a + n)))

    with nc.Block() as block:

        @block.sync
        def _(sp):
            sp.dma_start(raw[:, 0:1024].rearrange("p (o k) -> p o k", k=512),
                         w1.rearrange("(o p) k -> p o k", p=P)).then_inc(raw_loaded, 16)
            sp.dma_start(raw[:, 1024:1280], w2).then_inc(raw_loaded, 16)
            sp.dma_start(raw[:, 1280:1536].rearrange("p (o k) -> p o k", k=128),
                         w3.rearrange("(o p) k -> p o k", p=P)).then_inc(raw_loaded, 16)
            sp.dma_start(raw[:, 1536:2560].rearrange("p (o k) -> p o k", k=256),
                         w4.rearrange("(o p) k -> p o k", p=P)).then_inc(raw_loaded, 16)
            for c in range(4):
                sp.dma_start(x[:, 4 * c:4 * c + 4, :],
                             x2_dram[c * 512:(c + 1) * 512, :].rearrange("(t p) f -> p t f", p=P)
                             ).then_inc(x_loaded[c], 16)
            for c in range(4):
                sp.wait_ge(y_ready, CT * (c + 1))
                sp.dma_start(out[c * 512:(c + 1) * 512, :].rearrange("(t p) f -> p t f", p=P),
                             x[:, 4 * c:4 * c + 4, :]).then_inc(stored, 16)
            sp.wait_ge(stored, 64)

        @block.gpsimd
        def _(pool):
            pool.wait_ge(b_loaded, 64)
            for c in range(4):
                pool.wait_ge(x_loaded[c], 16)
                nc.gpsimd.tensor_tensor(x[:, CT * c:CT * c + CT, :], x[:, CT * c:CT * c + CT, :],
                                        b4[:, :].unsqueeze(1).to_broadcast([P, CT, F]), ALU.add).then_inc(xb_ready, 1)

        @block.scalar
        def _(act):
            act.dma_start(b_rows[0:2, :], b_drams[0].rearrange("(o p) -> o p", p=P)).then_inc(b_loaded, 16)
            act.dma_start(b_rows[2:3, :], b_drams[1].rearrange("(o p) -> o p", p=P)).then_inc(b_loaded, 16)
            act.dma_start(b_rows[3:5, :], b_drams[2].rearrange("(o p) -> o p", p=P)).then_inc(b_loaded, 16)
            act.dma_start(b4[:, :], b_drams[3].partition_broadcast(P)).then_inc(b_loaded, 16)

            def enc(it):
                act.wait_ge(turned, it + 1)
                if it >= 8 and it % CT == 0:
                    act.wait_ge(layer[0], 2 * (it // CT - 1))
                act.activation(enc_parts[0][:, it // CT % 2, :, rows(it % CT)],
                               ps[:, it % 2, :].rearrange("p (k i) -> p k i", i=P), ACT.Copy).then_inc(enc_high, 1)

            def hidden(c, n):
                for h in range(HALVES[n]):
                    act.wait_ge(layer[n], HALVES[n] * c + h + 1)
                    if c:
                        act.wait_ge(low[n], HALVES[n] * (c - 1) + h + 1)
                        if h == 0:
                            act.wait_ge(*((layer[1], c), (layer[2], 2 * c), (l4, CT * c))[n])
                    bias = b_col[:, BIAS[n] + h:BIAS[n] + h + 1]
                    for to in (o[n], o_parts[n][0]):
                        act.activation(to[:, h, :], ps[:, BANK[n][h], :], ACT.Relu, bias=bias).then_inc(high[n], 1)

            for it in (0, 1):
                enc(it)
            for k in range(5):
                act.wait_ge(w_turned, k + 1)
                act.activation(wH[:, rows(k, F)], ps[:, 2 + k, :], ACT.Copy).then_inc(w_high, 1)
            for it in (2, 3):
                enc(it)
            act.wait_ge(b_ready, 1)
            run(enc, hidden, lambda it: None)

        @block.vector
        def _(dve):
            def enc(it):
                dve.wait_ge(enc_high, it + 1)
                at = (slice(None), it // CT % 2, slice(None), rows(it % CT))
                nc.vector.tensor_tensor(enc_parts[1][at], ps[:, it % 2, :].rearrange("p (k i) -> p k i", i=P),
                                        enc_parts[0][at].bitcast(fp32), ALU.subtract).then_inc(enc_low, 1)

            def hidden(c, n):
                for h in range(HALVES[n]):
                    dve.wait_ge(high[n], 2 * (HALVES[n] * c + h + 1))
                    nc.vector.tensor_tensor(o_parts[n][1][:, h, :], o[n][:, h, :], o_parts[n][0][:, h, :].bitcast(fp32),
                                            ALU.subtract).then_inc(low[n], 1)

            def fourth(it):
                dve.wait_ge(l4, it + 1)
                dve.wait_ge(xb_ready, it // CT + 1)
                nc.vector.tensor_tensor(x[:, it, :], ps[:, BANK4[it % 2], :], x[:, it, :], ALU.add).then_inc(y_ready, 1)

            dve.wait_ge(b_turned, 1)
            nc.vector.tensor_copy(b_col[:, :], ps[:, 7, 0:5]).then_inc(b_ready, 1)
            for it in (0, 1):
                enc(it)
            for k in range(5):
                dve.wait_ge(w_high, k + 1)
                nc.vector.tensor_tensor(wL[:, rows(k, F)], ps[:, 2 + k, :], wH[:, rows(k, F)].bitcast(fp32),
                                        ALU.subtract).then_inc(w_ready, 1)
            for it in (2, 3):
                enc(it)
            run(enc, hidden, fourth)

        @block.tensor
        def _(pe):
            def enc(it):
                if it >= 2:
                    pe.wait_ge(enc_low, it - 1)
                for k in range(KT):
                    last = nc.tensor.transpose(ps[:, it % 2, rows(k)], v[:, it, rows(k)], ident[:, :])
                last.then_inc(turned, 1)

            def hidden(c, n):
                if c == 0:
                    pe.wait_ge(w_ready, (2, 3, 5)[n])
                if n == 0:
                    pe.wait_ge(enc_low, CT * (c + 1))
                else:
                    pe.wait_ge(low[n - 1], HALVES[n - 1] * (c + 1))
                for h in range(HALVES[n]):
                    if c:
                        pe.wait_ge(high[n], 2 * (HALVES[n] * (c - 1) + h + 1))
                    if n == 2 and h == 1 and c:
                        pe.wait_ge(y_ready, CT * c - 1)
                    left = ([w_at(W1 + 256 * k + P * h, P) for k in range(KT)], [w_at(W2 + P * k, P) for k in range(2)],
                            [w_at(W3 + P * h, P)])[n]
                    right = ([(enc_parts[0][:, c % 2, k, :], enc_parts[1][:, c % 2, k, :]) for k in range(KT)] if n == 0
                             else [(o_parts[n - 1][0][:, k, :], o_parts[n - 1][1][:, k, :])
                                   for k in range(HALVES[n - 1])])
                    split_matmul(nc, ps[:, BANK[n][h], :], left, right).then_inc(layer[n], 1)

            def fourth(it):
                if it % CT == 0:
                    pe.wait_ge(low[2], 2 * (it // CT + 1))
                if it >= 2:
                    pe.wait_ge(y_ready, it - 1)
                if it % CT == 0:
                    pe.wait_ge(high[2], 4 * (it // CT + 1))
                split_matmul(nc, ps[:, BANK4[it % 2], :],
                             [(o_parts[2][0][:, k, rows(it % CT)], o_parts[2][1][:, k, rows(it % CT)])
                              for k in range(2)],
                             [w_at(W4 + 512 * k, F) for k in range(2)]).then_inc(l4, 1)

            for it in (0, 1):
                enc(it)
            pe.wait_ge(b_loaded, 64)
            nc.tensor.transpose(ps[:, 7, 0:5], b_rows[:, :], ident[0:5, 0:5]).then_inc(b_turned, 1)
            pe.wait_ge(raw_loaded, 64)
            blocks = ([(W1 + 256 * k + P * h, 512 * h + P * k) for k in range(4) for h in range(2)]
                      + [(W2 + P * k, 1024 + P * k) for k in range(2)]
                      + [(W3 + P * h, 1280 + P * h) for h in range(2)]
                      + [(W4 + 512 * k + P * h, 1536 + 256 * h + P * k) for k in range(2) for h in range(4)])
            for n, (to, at) in enumerate(blocks):
                last = nc.tensor.transpose(ps[:, 2 + to // F, to % F:to % F + P], raw[:, at:at + P], ident[:, :])
                if n % 4 == 3:
                    last.then_inc(w_turned, 1)
            for it in (2, 3):
                enc(it)
            run(enc, hidden, fourth)


def build(nc, x, adj, w_seq, a1_0, a2_0, w_out, b_out, w_1, a1_1, a2_1, w1, b1, w2, b2, w3, b3, w4, b4, out):
    with ExitStack() as ctx:
        def sem(name):
            return ctx.enter_context(nc.semaphore(name))

        def allocator(stack, tag):
            return lambda name, shape, dt=fp32: stack.enter_context(nc.sbuf_tensor(f"{tag}{name}", shape, dt))

        keep = allocator(ctx, "")
        s1_rows = [nc.dram_tensor(f"s1_rows{n}", [h, N], fp32, kind="Internal").ap() for n, h in enumerate((16, 8))]
        x2_dram = nc.dram_tensor("x2", [N, F], fp32, kind="Internal").ap()
        ps = ctx.enter_context(nc.psum_tensor("ps", [P, 8, F], fp32))
        mask = keep("mask", [P, NT, N], u8)
        v = keep("v", [P, NT, 16 * 33])
        ident = keep("ident", [P, P])
        e_col = keep("e_col", [P, NT])
        half = keep("half", [P, 2])
        v0, v1 = v[:, :, 0:16 * 33], v[:, :, 0:8 * 65]
        sc = keep("sc", [P, NT, SC])
        mean = sc[:, :, :].rearrange("p t c -> p (t c)")

        def transform_parts(own):
            return dict(
                w_parts=[own(f"w{n}", [P, KT, F], fp32r) for n in range(2)],
                prod=own("prod", [P, 2 * KT, F]), wa=own("wa", [P, KT, SC]),
                wa_parts=own("wa_parts", [P, KT, 2, SC], fp32r),
                xs=own("xs", [P, 4, F]), xn=own("xn", [P, 2, F]),
                h_parts=[own(f"h{n}", [P, 2, KT, P], fp32r) for n in range(2)],
                stats=own("stats", [P, 2, 6]), mv=own("mv", [P, 2, 2]), var_eps=own("var_eps", [P, 2, 1]),
                rstd=own("rstd", [P, 2, 1]))

        def attend(n, tag, H, D, dve_tiles, vv, **more):
            with ExitStack() as part:
                own = allocator(part, tag)
                small = [own("bd", [P, 2, NT, H]), own("ratio", [P, NT, H]), own("neg_s2", [P, NT, H])]
                sums = own("sums", [P, NT, 2 * (D + 1)])
                flat = sums[:, :, :].rearrange("p t c -> p (t c)")
                cut = lambda at: flat[:, at:at + NT * H].rearrange("p (t h) -> p t h", h=H)
                small += [cut(0), cut(NT * H), own("gm", [P, H + 1]), own("g", [P, H]),
                          own("shift", [P, 2, 2, NT]), own("one_minus_e", [P, NT])]
                s_rows = flat[:, 512:1024]
                if n:
                    more["mean_w"] = flat[:, 1024:1024 + P]
                attention(nc, tag, H, D, dve_tiles, mask, vv, sc, small, s_rows, s1_rows[n],
                          own("t_buf", [P, 2, NT, HALF], u8), own("u_buf", [P, 2, NT, HALF], u8),
                          own("s1", [P, 2, N]), own("parts", [P, 2, 2, NT, D + 1, 3]), sums, ident, ps, sem, **more)

        with ExitStack() as part:
            own = allocator(part, "t_")
            first_transform(nc, "t", x, adj, [w_seq[rows(kt), :].rearrange("p (h d) -> p h d", d=32) for kt in range(KT)],
                            (a1_0, a2_0), v0, mask, e_col, w=own("w", [P, KT, F]), a_bc=own("a_bc", [P, 2, 32]),
                            adj=own("adj", [P, 4, N]), adj_b=own("adj_b", [P, 2, N], bf16),
                            ident_b=own("ident_b", [P, P], bf16), deg=own("deg", [P, 2, 1]),
                            half=half[:, 0:1], sc=sc, ident=ident, ps=ps, sem=sem, **transform_parts(own))
        with ExitStack() as part:
            own = allocator(part, "n_")
            out_w, out_b, w = own("out_w", [P, KT, F]), own("out_b", [P, F]), own("w", [P, KT, F])
            a_bc = own("a_bc", [P, 2, F])
            prefetch = [(out_w[:, :, :], w_out.rearrange("(k p) n -> p k n", p=P)),
                        (out_b[:, :], b_out.partition_broadcast(P)),
                        (a_bc[:, 0, :], a1_1.rearrange("h d -> (h d)").partition_broadcast(P)),
                        (a_bc[:, 1, :], a2_1.rearrange("h d -> (h d)").partition_broadcast(P))]
            prefetch += [(w[:, kt, :].rearrange("p (h d) -> p h d", d=64), w_1[:, rows(kt), :].rearrange("h p d -> p h d"))
                         for kt in range(KT)]
            attend(0, "a0", 16, 32, (7, 15), v0, prefetch=prefetch)
            own = allocator(part, "m_")
            middle(nc, "m", x, x2_dram, v0, out_w, [own(f"out{n}", [P, KT, F], fp32r) for n in range(2)], out_b, w=w,
                   a_bc=a_bc, vt=own("vt", [P, 2, F]), a_parts=[own(f"a{n}", [P, 2, KT, P], fp32r) for n in range(2)],
                   z=own("z", [P, 2, F]), e=own("e", [P, 2, F]), half=half, sc=sc, v2=v1, ident=ident, ps=ps, sem=sem,
                   **transform_parts(own))
        attend(1, "a1", 8, 64, (15,), v1, e_col=e_col, mean=mean)
        with ExitStack() as part:
            own = allocator(part, "p_")
            mlp(nc, "p", own("x", [P, NT, F]), x2_dram, out, (w1, w2, w3, w4), (b1, b2, b3, b4),
                own("raw", [P, 2560]), [own(f"wT{n}", [P, 2560], fp32r) for n in range(2)], own("b_rows", [5, P]),
                own("b_col", [P, 5]), own("b4", [P, F]), v1, [own(f"enc{n}", [P, 2, KT, F], fp32r) for n in range(2)],
                [own(f"o{n}", [P, (2, 1, 2)[n], F]) for n in range(3)],
                [[own(f"o{n}{m}", [P, (2, 1, 2)[n], F], fp32r) for m in range(2)] for n in range(3)], ident, ps, sem)


NAMES = ["x", "adj", "L0_gnn_W_seq", "L0_gnn_a1", "L0_gnn_a2", "L0_gnn_W_out", "L0_gnn_b_out", "L1_gnn_W",
         "L1_gnn_a1", "L1_gnn_a2", "L1_gnn_W1", "L1_gnn_b1", "L1_gnn_W2", "L1_gnn_b2", "L1_gnn_W3", "L1_gnn_b3",
         "L1_gnn_W4", "L1_gnn_b4"]


def kernel(**inputs):
    import numpy as np
    import concourse.bacc as bacc
    from concourse.bass_utils import run_bass_kernel_spmd

    nc = bacc.Bacc("TRN2", target_bir_lowering=False, num_devices=1)
    arrays, args = {}, []
    for name in NAMES:
        a = np.ascontiguousarray(inputs[name])
        arrays["in_" + name] = a
        args.append(nc.dram_tensor("in_" + name, a.shape, mybir.dt.from_np(a.dtype), kind="ExternalInput").ap())
    out = nc.dram_tensor("out_0", (N, F), fp32, kind="ExternalOutput").ap()
    build(nc, *args, out)
    r = run_bass_kernel_spmd(nc, [arrays], core_ids=[0])
    return r.results[0]["out_0"]
```

```python
import concourse.bass as bass
from concourse import mybir
from contextlib import ExitStack

fp32 = mybir.dt.float32
fp32r = mybir.dt.float32r
bf16 = mybir.dt.bfloat16
fp8 = mybir.dt.float8e4
u8 = mybir.dt.uint8
i8 = mybir.dt.int8
u16 = mybir.dt.uint16
ALU = mybir.AluOpType
ACT = mybir.ActivationFunctionType
AX = mybir.AxisListType
RMAX = bass.bass_isa.ReduceOp.max

P = 128
N = 2048
F = 512
NT = N // P
KT = F // P
ONE8 = 56
S2 = 16
SC = 32
LIFT = 60.0
SLOPE = 0.2
EPS = 1e-5


def rows(it, n=P):
    return slice(it * n, (it + 1) * n) if isinstance(it, int) else bass.ds(it * n, n)


def wait_from(eng, sem, value):
    if not isinstance(value, int) or value > 0:
        eng.wait_ge(sem, value)


def pipeline(eng, step, end, first, last, unroll):
    for s in range(first):
        step(s, s)
    with eng.Fori(0, (last - first) // unroll) as m:
        for k in range(first, first + unroll):
            step(unroll * m + k, k)
    for s in range(last, end):
        step(s, s)


def has_tile(t):
    return not isinstance(t, int) or 0 <= t < NT


def tile_of(ap, t):
    return ap[:, t, :] if isinstance(t, int) else ap[:, bass.ds(t, 1), :].rearrange("p a f -> p (a f)")


def split_matmul(nc, out, left, right):
    n = len(left)
    for k in range(n):
        (lh, ll), (rh, rl) = left[k], right[k]
        nc.tensor.matmul(out, lh, rh, start=(k == 0), stop=False)
        nc.tensor.matmul(out, lh, rl, start=False, stop=False)
        last = nc.tensor.matmul(out, ll, rh, start=False, stop=(k == n - 1))
    return last


def score_matmul(nc, out, left, wa_parts):
    n = len(left)
    for k in range(n):
        high = (out[:, 0:2 * SC], left[k][0], wa_parts[:, k, :, :].rearrange("p a c -> p (a c)"))
        low = (out[:, 0:SC], left[k][1], wa_parts[:, k, 0, :])
        for at, stationary, moving in ((high, low) if k < n - 1 else (low, high)):
            last = nc.tensor.matmul(at, stationary, moving, start=(k == 0 and at is high[0]),
                                    stop=(k == n - 1 and at is high[0]))
    return last


def take_scores(nc, to, sums):
    return nc.vector.tensor_reduce(to, sums[:, 0:2 * SC].rearrange("p (a c) -> p c a", a=2), AX.X, ALU.add)


def attention(nc, tag, H, D, UNITS, m_chunks, dve_tiles, first_dve_tiles, mask, v, sc, small, s_rows, s1_rows, t_buf, u_buf, s1,
              parts, sums, ident, ps, sem, e_col=None, mean=None, mean_w=None, prefetch=(), prefetch_late=()):
    D1 = D + 1
    W3 = 3 * D1
    PAIRS = H // 2
    bd, ratio, neg_s2, sh, zr, gm, g, shift, one_minus_e = small
    act_tiles = [jt for jt in range(NT) if jt not in dve_tiles]
    NA, ND = len(act_tiles), len(dve_tiles)
    QN, QT = N // UNITS, NT // UNITS
    NG = QT // 4
    TW = 8 * F // QT
    CH = 2 * UNITS
    NC = NT // CH
    CHUNKS = 8
    NU = NC - len(m_chunks)
    MT = CH * len(m_chunks)
    EXTRA = len(first_dve_tiles)
    WEIGHT_STEPS = 4 if MT else 3
    SPLIT_AT = ((), (), (), (0,), (), (1,), (2,), (3,)) if mean is None else ((), (), (), (), (), (0,), (1,), (2, 3))
    STEPS = 4 if mean is None else 3
    psum = ps[:, :, :].rearrange("p b c -> p (b c)")

    def own_rank(jt, chunks):
        return CH * chunks.index(jt // CH) + jt % CH

    u_chunks = [c for c in range(NC) if c not in m_chunks]

    s1_loaded = [sem(f"{tag}_s1_loaded{b}") for b in range(2)]
    act_shift = sem(tag + "_act_shift")
    dve_shift = sem(tag + "_dve_shift")
    waits_over = sem(tag + "_waits_over")
    act_compared = sem(tag + "_act_compared")
    dve_compared = sem(tag + "_dve_compared")
    first_compared = sem(tag + "_first_compared")
    extra_compared = sem(tag + "_extra_compared")
    t_ready = sem(tag + "_t_ready")
    u_ready = sem(tag + "_u_ready")
    weighted = sem(tag + "_weighted")
    parts_ready = sem(tag + "_parts_ready")
    chunk_done = sem(tag + "_chunk_done")
    group_done = sem(tag + "_group_done")
    group_free = sem(tag + "_group_free")
    post = sem(tag + "_post")

    max_ready = sem(tag + "_max_ready")
    lifted = sem(tag + "_lifted")
    neg_ready = sem(tag + "_neg_ready")
    shifted = sem(tag + "_shifted")
    exps = sem(tag + "_exps")
    sc_turned = sem(tag + "_sc_turned")
    s_rows_ready = sem(tag + "_s_rows_ready")
    rows_stored = sem(tag + "_rows_stored")
    s1_begun = sem(tag + "_s1_begun")
    if mean is not None:
        z_ready = sem(tag + "_z_ready")
        exp_ready = sem(tag + "_exp_ready")
        elu_ready = sem(tag + "_elu_ready")
        mean_summed = sem(tag + "_mean_summed")
        mean_ready = sem(tag + "_mean_ready")
    prefetched = sem(tag + "_prefetched")

    def part_tiles(part):
        return slice(0, NT) if part is None else slice(NT // 2 * part, NT // 2 * (part + 1))

    GQ = QT // (P // SC)

    def first_row(n):
        tiles = s1[:, 0, 0:QN].rearrange("p (g l q) -> p l g q", l=P // SC, q=P)
        return tiles[:, 2 * n:2 * n + 2, :, :]

    def first_sums(n):
        return psum[:, F + n * QN // 2:F + (n + 1) * QN // 2].rearrange("p (l g q) -> p l g q", l=2, q=P)

    def loaded_count(m, b):
        return 16 * m if b == 0 and QN == N else 16 * m + 16

    with nc.Block() as block:

        @block.sync
        def _(sp):
            def load(h, b):
                sp.dma_start(s1[:, b, :], s1_rows[h:h + 1, :].rearrange("a n -> (a n)").partition_broadcast(P)
                             if isinstance(h, int) else
                             s1_rows[bass.ds(h, 1), :].rearrange("a n -> (a n)").partition_broadcast(P)
                             ).then_inc(s1_loaded[b], 16)

            per = P // SC
            view = s1_rows.rearrange("c (g l p) -> l c g p", l=per, p=P)
            sp.wait_ge(s_rows_ready, 1)
            for t in range(per):
                sp.dma_start(view[t], s_rows[SC * t:SC * t + H, :].rearrange("c (g p) -> c g p", p=P)
                             ).then_inc(rows_stored, 16)
            sp.wait_ge(rows_stored, 16 * per)
            if QN < N:
                sp.dma_start(s1[:, 0, QN:N], s1_rows[0, QN:N].partition_broadcast(P)).then_inc(s1_loaded[0], 16)
            load(1, 1)
            for dst, src in prefetch:
                sp.dma_start(dst, src).then_inc(prefetched, 16)
            with sp.Fori(0, PAIRS - 1) as m:
                for b in range(2):
                    sp.wait_ge(t_ready, 2 * CHUNKS * m + CHUNKS * (b + 1))
                    load(2 * m + 2 + b, b)
            sp.wait_ge(t_ready, CHUNKS * H)
            for dst, src in prefetch_late:
                sp.dma_start(dst, src).then_inc(prefetched, 16)
            sp.wait_ge(prefetched, 16 * (len(prefetch) + len(prefetch_late)))

        @block.gpsimd
        def _(pool):
            nc.gpsimd.memset(gm[:, H:H + 1], LIFT).then_inc(lifted, 1)
            if mean is not None:
                nc.gpsimd.memset(mean_w, 1.0 / N).then_inc(lifted, 1)
            pool.wait_ge(neg_ready, 1)
            nc.gpsimd.partition_all_reduce(g[:, :], gm[:, 0:H], P, RMAX).then_inc(max_ready, 1)

        @block.scalar
        def _(act):
            act.wait_ge(sc_turned, 1)
            act.activation(s_rows[:, :], ps[:, 0, :], ACT.Copy).then_inc(s_rows_ready, 1)
            act.wait_ge(sc_turned, 2)
            act.activation(first_row(0), first_sums(0), ACT.Copy).then_inc(s1_begun, 1)
            act.wait_ge(shifted, 1)
            act.wait_ge(lifted, 1)
            lift = gm[:, H:H + 1]
            act.activation(bd[:, 0, :, :], sh[:, :, :], ACT.Exp, bias=lift).then_inc(exps, 1)
            act.activation(bd[:, 1, :, :], sh[:, :, :], ACT.Exp, scale=SLOPE).then_inc(exps, 1)
            act.wait_ge(shifted, 3)
            act.activation(ratio[:, :, :], zr[:, :, :], ACT.Exp, scale=SLOPE - 1.0, bias=lift).then_inc(exps, 1)
            act.wait_ge(neg_ready, 2)
            def exp_output(h, part=None):
                its = part_tiles(part)
                act.wait_ge(z_ready, 4 * (h + 1 if part == 1 else h) + 4)
                act.activation(sums[:, its, D1 + 1:2 * D1], sums[:, its, 0:D], ACT.Exp).then_inc(exp_ready, 1)

            def unit(m, b, half, first=False):
                u = 2 * UNITS * m + UNITS * b + half
                first_unit = first and b == 0 and half == 0
                if half == 0:
                    h = 2 * m + b
                    hs = slice(h, h + 1) if isinstance(m, int) else bass.ds(h, 1)
                    act.activation(shift[:, 0, b, :].unsqueeze(2), neg_s2[:, :, hs], ACT.Copy).then_inc(act_shift, 1)
                    act.wait_ge(act_shift, 2 * m + b + 1)
                if first_unit:
                    act.wait_ge(s1_begun, 2)
                elif half == 0 or (first and b == 0):
                    act.wait_ge(s1_loaded[b], loaded_count(m, b))
                for c in range(NC):
                    if c < NC - 1:
                        act.wait_ge(chunk_done, (NC - 1) * u + c + 1)
                    else:
                        act.wait_ge(group_done, NG * u + NG)
                    for jt in range(CH * c, CH * (c + 1)):
                        if jt not in act_tiles or (first_unit and jt in first_dve_tiles):
                            continue
                        act.activation(t_buf[:, half, jt, :].bitcast(i8), s1[:, b, half * QN:(half + 1) * QN],
                                       ACT.Sign, bias=shift[:, 0, b, jt:jt + 1], scale=-1.0
                                       ).then_inc(first_compared if first_unit else act_compared, 1)
                    if mean is not None and half == 1 and c == 0 and (b or not first):
                        exp_output(2 * m + b - 1)
                if first_unit:
                    act.sem_inc(act_compared, NA)

            for b in range(2):
                for half in range(UNITS):
                    unit(0, b, half, first=True)
            with act.Fori(0, PAIRS - 1) as m:
                for b in range(2):
                    for half in range(UNITS):
                        unit(m + 1, b, half)
            if mean is not None:
                exp_output(H - 1, part=0)
                exp_output(H - 1, part=1)

        @block.vector
        def _(dve):
            def split_values(m, b, steps):
                h = 2 * m + b
                w = parts[:, b, 0:2 * NT, :, :]
                for c in steps:
                    if c == 0:
                        src = v[:, :, h * D1:(h + 1) * D1] if isinstance(h, int) else v[:, :, bass.ds(h * D1, D1)]
                        f = bd[:, :, :, h:h + 1] if isinstance(h, int) else bd[:, :, :, bass.ds(h, 1)]
                        nc.vector.tensor_tensor(w[:, :, :, 0].rearrange("p (x t) d -> p x t d", x=2),
                                                src.unsqueeze(1).to_broadcast([P, 2, NT, D1]),
                                                f.to_broadcast([P, 2, NT, D1]), ALU.mult).then_inc(weighted, 1)
                    elif c < 3:
                        dve.wait_ge(weighted, WEIGHT_STEPS * h + c)
                        nc.vector.tensor_tensor(w[:, :, :, c], w[:, :, :, c - 1], w.bitcast(bf16)[:, :, :, 2 * c - 1],
                                                ALU.subtract).then_inc(weighted, 1)
                    else:
                        if MT:
                            dve.wait_ge(weighted, WEIGHT_STEPS * h + 3)
                            every_other = lambda ap: ap.rearrange("p (n x c) d e -> p n x (c d e)", x=2, c=CH)[:, 0:MT // CH, 0, :]
                            nc.vector.tensor_scalar(
                                parts[:, b, 2 * NT:2 * NT + MT, :, :].rearrange("p (n c) d e -> p n (c d e)", c=CH),
                                every_other(parts[:, b, NT:2 * NT, :, :]), -1.0, None, ALU.mult).then_inc(weighted, 1)
                        dve.wait_ge(weighted, WEIGHT_STEPS * (h + 1))
                        dve.sem_inc(parts_ready, 1)

            def take_shift(m, b):
                h = 2 * m + b
                hs = slice(h, h + 1) if isinstance(h, int) else bass.ds(h, 1)
                nc.vector.tensor_copy(shift[:, 1, b, :].unsqueeze(2), neg_s2[:, :, hs]).then_inc(dve_shift, 1)

            def compare(m, b, half, c):
                first_unit = isinstance(m, int) and m == 0 and b == 0 and half == 0
                if UNITS == 1 and c < NC - 1 and any(jt // CH == c for jt in dve_tiles):
                    dve.wait_ge(chunk_done, (NC - 1) * (2 * m + b) + c + 1)
                for tiles, done in ((dve_tiles, dve_compared), (first_dve_tiles, extra_compared)):
                    if tiles is first_dve_tiles and not first_unit:
                        continue
                    for jt in tiles:
                        if CH * c <= jt < CH * (c + 1):
                            nc.vector.tensor_scalar(t_buf[:, half, jt, :], s1[:, b, half * QN:(half + 1) * QN],
                                                    shift[:, 1, b, jt:jt + 1], float(ONE8), ALU.is_gt,
                                                    ALU.mult).then_inc(done, 1)

            words = lambda ap: ap.bitcast(u16)

            def masks(m, b, half, c):
                u = 2 * UNITS * m + UNITS * b + half
                jts = slice(c * CH, (c + 1) * CH)
                t = words(t_buf[:, half, jts, :])
                mk = words(mask[:, jts, half * QN:(half + 1) * QN])
                first_unit = isinstance(u, int) and u == 0
                na = sum(jt < (c + 1) * CH and not (first_unit and jt in first_dve_tiles) for jt in act_tiles)
                nd = sum(jt < (c + 1) * CH for jt in dve_tiles)
                if first_unit:
                    dve.wait_ge(first_compared, na)
                    ne = sum(jt < (c + 1) * CH for jt in first_dve_tiles)
                    if ne:
                        dve.wait_ge(extra_compared, ne)
                else:
                    dve.wait_ge(act_compared, NA * u + na)
                if nd:
                    dve.wait_ge(dve_compared, ND * u + nd)
                nc.vector.tensor_tensor(t, t, mk, ALU.bitwise_and).then_inc(t_ready, 1)

            def rest(m, b, half, c):
                u = 2 * UNITS * m + UNITS * b + half
                if c in m_chunks:
                    return
                jts = slice(c * CH, (c + 1) * CH)
                at = CH * u_chunks.index(c)
                dve.wait_ge(t_ready, NC * u + c + 1)
                nc.vector.tensor_tensor(words(u_buf[:, half, at:at + CH, :]), words(t_buf[:, half, jts, :]),
                                        words(mask[:, jts, half * QN:(half + 1) * QN]),
                                        ALU.bitwise_xor).then_inc(u_ready, 1)

            def drain(u, half, g):
                dve.wait_ge(group_done, NG * u + g + 1 + NG * UNITS)
                it = half * QT + 4 * g
                nc.vector.tensor_reduce(sums[:, it:it + 4, :],
                                        psum[:, 4 * g * TW:4 * (g + 1) * TW].rearrange("p (k w) -> p k w", w=TW)
                                        [:, :, 0:2 * W3].rearrange("p k (m c) -> p k m c", c=3),
                                        AX.X, ALU.add).then_inc(group_free, 1)

            def normalise(m, b, steps=range(4), part=None):
                h = 2 * m + b
                hs = slice(h, h + 1) if isinstance(h, int) else bass.ds(h, 1)
                vs = slice(h * D, h * D + D) if isinstance(h, int) else bass.ds(h * D, D)
                its = part_tiles(part)
                nt = its.stop - its.start
                turn = h + 1 if part == 1 else h
                if 0 in steps:
                    dve.wait_ge(group_free, 4 * h + (2 if part == 0 else 4) + NG)
                    nc.vector.tensor_tensor(sums[:, its, D1:2 * D1], sums[:, its, D1:2 * D1],
                                            ratio[:, its, hs].to_broadcast([P, nt, D1]), ALU.mult).then_inc(post, 1)
                if 1 in steps:
                    dve.wait_ge(post, STEPS * turn + 1)
                    nc.vector.tensor_tensor(sums[:, its, 0:D1], sums[:, its, 0:D1], sums[:, its, D1:2 * D1],
                                            ALU.add).then_inc(post, 1)
                if 2 in steps:
                    dve.wait_ge(post, STEPS * turn + 2)
                    nc.vector.reciprocal(sums[:, its, D1:D1 + 1], sums[:, its, D:D1]).then_inc(post, 1)
                    if mean is not None:
                        nc.vector.tensor_tensor(sums[:, its, D1 + 1:2 * D1],
                                                mean[:, vs].unsqueeze(1).to_broadcast([P, nt, D]),
                                                e_col[:, its].unsqueeze(2).to_broadcast([P, nt, D]),
                                                ALU.mult).then_inc(z_ready, 1)
                        dve.wait_ge(post, STEPS * turn + 3)
                        nc.vector.tensor_tensor(sums[:, its, D1:D1 + 1], sums[:, its, D1:D1 + 1],
                                                one_minus_e[:, its].unsqueeze(2), ALU.mult).then_inc(z_ready, 1)
                if 3 in steps:
                    by = sums[:, its, D1:D1 + 1].to_broadcast([P, nt, D])
                    if mean is None:
                        dve.wait_ge(post, STEPS * turn + 3)
                        nc.vector.tensor_tensor(v[:, its, vs], sums[:, its, 0:D], by, ALU.mult).then_inc(post, 1)
                        return
                    dve.wait_ge(z_ready, 4 * turn + 2)
                    nc.vector.tensor_tensor(sums[:, its, 0:D], sums[:, its, 0:D], by, ALU.mult).then_inc(z_ready, 1)
                    dve.wait_ge(z_ready, 4 * turn + 3)
                    nc.vector.tensor_tensor(sums[:, its, 0:D], sums[:, its, 0:D], sums[:, its, D1 + 1:2 * D1],
                                            ALU.add).then_inc(z_ready, 1)

            def elu(m, b, part=None):
                h = 2 * m + b
                vs = slice(h * D, h * D + D) if isinstance(h, int) else bass.ds(h * D, D)
                its = part_tiles(part)
                turn = h + 1 if part == 1 else h
                dve.wait_ge(exp_ready, turn + 1)
                nc.vector.tensor_scalar(sums[:, its, D1 + 1:2 * D1], sums[:, its, D1 + 1:2 * D1], 1.0, -1.0, ALU.min,
                                        ALU.add).then_inc(elu_ready, 1)
                dve.wait_ge(elu_ready, 2 * turn + 1)
                nc.vector.tensor_tensor(v[:, its, vs], sums[:, its, 0:D], sums[:, its, D1 + 1:2 * D1],
                                        ALU.max).then_inc(elu_ready, 1)
                dve.wait_ge(elu_ready, 2 * turn + 2)

            def head(m, b, first=False, last=False):
                before = b or not first
                after = not (last and b)
                head_before, head_after = (m if b else m - 1, 1 - b), (m + b, 1 - b)
                for n in range(CHUNKS):
                    half, c = n // NC, n % NC
                    first_unit = not before and half == 0
                    if c == 0 and (ND or first_unit):
                        if half == 0:
                            dve.wait_ge(dve_shift, 2 * m + b + 1)
                        if first_unit:
                            dve.wait_ge(s1_begun, 2)
                        elif half == 0 or not before:
                            dve.wait_ge(s1_loaded[b], loaded_count(m, b))
                    if c == 0:
                        compare(m, b, half, 0)
                    masks(m, b, half, c)
                    if c < NC - 1:
                        if not (first_unit and c == 0):
                            compare(m, b, half, c + 1)
                    elif half == UNITS - 1 and ND and after:
                        take_shift(*head_after)
                    if before and n == 2:
                        normalise(*head_before, steps=(1,))
                    elif before and n == 3 and mean is None:
                        normalise(*head_before, steps=(3,))
                    rest(m, b, half, c)
                    if first_unit and c == 0:
                        if mean is not None:
                            dve.wait_ge(mean_summed, 1)
                            nc.vector.tensor_copy(mean[:, :], ps[:, 0, :]).then_inc(mean_ready, 1)
                            dve.wait_ge(neg_ready, 3)
                            dve.wait_ge(mean_ready, 1)
                        dve.wait_ge(s_rows_ready, 1)
                        dve.sem_inc(group_free, NG)
                        compare(m, b, half, 1)
                    if mean is not None and before and n == NC:
                        elu(*head_before)
                    if c == 1 and not first_unit:
                        u = 2 * UNITS * m + UNITS * b + half - 1
                        for g in range(NG):
                            drain(u, (half - 1) % UNITS, g)
                    if before and n == 1:
                        normalise(*head_before, steps=(0,))
                    elif before and n == 2:
                        normalise(*head_before, steps=(2,) if mean is None else (2, 3))
                    if after:
                        split_values(*head_after, steps=SPLIT_AT[n])

            nc.vector.tensor_reduce(gm[:, 0:H], sc[:, :, S2:S2 + H].rearrange("p t h -> p h t"), AX.X,
                                    ALU.max).then_inc(neg_ready, 1)
            nc.vector.tensor_scalar(neg_s2[:, :, :], sc[:, :, S2:S2 + H], -1.0, None, ALU.mult).then_inc(neg_ready, 1)
            if e_col is not None:
                nc.vector.tensor_scalar(one_minus_e[:, :], e_col[:, :], -1.0, 1.0, ALU.mult,
                                        ALU.add).then_inc(neg_ready, 1)
            dve.wait_ge(neg_ready, 2)
            take_shift(0, 0)
            dve.wait_ge(sc_turned, 2)
            nc.vector.tensor_copy(first_row(1), first_sums(1)).then_inc(s1_begun, 1)
            dve.wait_ge(max_ready, 1)
            gb = g[:, :].unsqueeze(1).to_broadcast([P, NT, H])
            nc.vector.tensor_tensor(sh[:, :, :], sc[:, :, S2:S2 + H], gb, ALU.subtract).then_inc(shifted, 1)
            nc.vector.tensor_tensor(zr[:, :, :], sc[:, :, 0:H], gb, ALU.add).then_inc(shifted, 1)
            dve.wait_ge(shifted, 2)
            nc.vector.tensor_scalar(zr[:, :, :], zr[:, :, :], 0.0, None, ALU.max).then_inc(shifted, 1)
            dve.wait_ge(exps, 3)
            split_values(0, 0, range(4))
            for b in range(2):
                head(0, b, first=True)
            with dve.Fori(0, PAIRS - 2) as m:
                for b in range(2):
                    head(m + 1, b)
            for b in range(2):
                head(PAIRS - 1, b, last=True)
            for part in range(2):
                if UNITS == 1 or part == 1:
                    for group in range(2):
                        drain(UNITS * H - 1, UNITS - 1, group + (2 * part if UNITS == 1 else 0))
                normalise(PAIRS - 1, 1, part=part)
                if mean is not None:
                    elu(PAIRS - 1, 1, part=part)

        @block.tensor
        def _(pe):
            pe.sem_inc(group_done, NG * UNITS)
            pe.sem_inc(chunk_done, UNITS * (NC - 1))
            per = P // SC
            for gq in range(NT // per):
                last = nc.tensor.transpose(ps[:, 0, rows(gq)],
                                           sc[:, per * gq:per * gq + per, :].rearrange("p t c -> p (t c)"),
                                           ident[:, :])
            last.then_inc(sc_turned, 1)
            pe.wait_ge(s_rows_ready, 1)
            for l in range(per):
                last = nc.tensor.matmul(psum[:, F + GQ * P * l:F + GQ * P * (l + 1)],
                                        ident[:, l * SC:l * SC + 1].to_broadcast([P, P]), s_rows[:, 0:GQ * P],
                                        start=True, stop=True)
            last.then_inc(sc_turned, 1)
            if mean is not None:
                pe.wait_ge(lifted, 2)
                pe.wait_ge(s_rows_ready, 1)
                for jt in range(NT):
                    last = nc.tensor.matmul(ps[:, 0, :], mean_w,
                                            v[:, jt, :].rearrange("p (h d) -> p h d", d=D1)[:, :, 0:D],
                                            start=(jt == 0), stop=(jt == NT - 1))
                last.then_inc(mean_summed, 1)
            def moving(b, at):
                return parts[:, b, at, :, :].rearrange("p x d c -> p x (d c)").bitcast(bf16)[:, :, 1::2]

            def unit(m, b, half):
                u = 2 * UNITS * m + UNITS * b + half
                if half == 0:
                    pe.wait_ge(parts_ready, 2 * m + b + 1)
                for c in range(NC):
                    if c in m_chunks:
                        pe.wait_ge(t_ready, NC * u + c + 1)
                    else:
                        pe.wait_ge(u_ready, NU * u + u_chunks.index(c) + 1)
                    for g in range(NG):
                        if c == 0:
                            pe.wait_ge(group_free, NG * u + g + 1)
                        if c == 0 or g == 0:
                            pe.sem_inc(waits_over, 1)
                        for it in range(4 * g, 4 * g + 4):
                            query = slice(half * QN + it * P, half * QN + (it + 1) * P)
                            first_in_bank = it * TW % F == 0
                            last_in_bank = (it + 1) * TW % F == 0
                            for jt in range(CH * c, CH * (c + 1)):
                                t_tile = t_buf[:, half, jt, rows(it)].bitcast(fp8)
                                if c in m_chunks:
                                    minus = 2 * NT + own_rank(jt, m_chunks)
                                    out_t = psum[:, it * TW:it * TW + 2 * W3]
                                    t_values = moving(b, slice(jt, minus + 1, minus - jt))
                                    others = mask[:, jt, query].bitcast(fp8)
                                else:
                                    out_t = psum[:, it * TW:it * TW + W3]
                                    t_values = moving(b, slice(jt, jt + 1))
                                    others = u_buf[:, half, own_rank(jt, u_chunks), rows(it)].bitcast(fp8)
                                nc.tensor.matmul(out_t, t_tile, t_values, start=(jt == 0 and first_in_bank), stop=False)
                                last = nc.tensor.matmul(psum[:, it * TW + W3:it * TW + 2 * W3], others,
                                                        moving(b, slice(NT + jt, NT + jt + 1)),
                                                        start=False, stop=(jt == NT - 1 and last_in_bank))
                        if c == NC - 1:
                            last.then_inc(group_done, 1)
                    if c < NC - 1:
                        last.then_inc(chunk_done, 1)

            with pe.Fori(0, PAIRS) as m:
                for b in range(2):
                    for half in range(UNITS):
                        unit(m, b, half)


def layer_norm_stats(nc, dve, x, b, stats, mv, var_eps, sems, t):
    stats_ready, stats_seen, mean_ready, var_ready = sems
    nc.vector.bn_stats(stats[:, b, :], x).then_inc(stats_ready, 1)
    dve.wait_ge(stats_ready, t + 1)
    dve.sem_inc(stats_seen, 1)
    nc.vector.bn_aggr(mv[:, b, :], stats[:, b, :]).then_inc(mean_ready, 1)
    dve.wait_ge(mean_ready, t + 1)
    nc.vector.tensor_scalar(var_eps[:, b, :], mv[:, b, 1:2], EPS, None, ALU.add).then_inc(var_ready, 1)


def attention_vectors(nc, tag, H, D, HA, w, w_parts, a_bc, prod, wa, wa_parts, sem, loads):
    if loads:
        loaded = sem(tag + "_wa_loaded")
    products = sem(tag + "_wa_products")
    wa_ready = sem(tag + "_wa_ready")
    high = sem(tag + "_w_high")
    split = sem(tag + "_w_split")
    PARTS = KT + 2

    def load(eng, w_dram, a_dram):
        for kt in range(KT):
            eng.dma_start(w[:, kt, :].rearrange("p (h d) -> p h d", d=D), w_dram[kt]).then_inc(loaded, 16)
        for a, src in enumerate(a_dram):
            eng.dma_start(a_bc[:, a, :], src.partition_broadcast(P)).then_inc(loaded, 16)

    def product(eng, a, k0, k1):
        vec = a_bc[:, a, :].rearrange("p (h d) -> p h d", d=D)
        n = k1 - k0
        if n == 1:
            vec = vec.to_broadcast([P, H, D]) if HA == 1 else vec
            at, by = prod[:, KT * a + k0, :], w[:, k0, :]
            at, by = (ap.rearrange("p (h d) -> p h d", d=D) for ap in (at, by))
        else:
            vec = vec.unsqueeze(1).to_broadcast([P, n, H, D])
            at, by = prod[:, KT * a + k0:KT * a + k1, :], w[:, k0:k1, :]
            at, by = (ap.rearrange("p k (h d) -> p k h d", d=D) for ap in (at, by))
        return eng.tensor_tensor(at, by, vec, ALU.mult)

    def pool_part(pool):
        nc.gpsimd.memset(wa[:, :, :], 0.0).then_inc(products, 1)
        if loads:
            pool.wait_ge(loaded, 16 * PARTS)
        for k in range(KT):
            product(nc.gpsimd, 0, k, k + 1).then_inc(products, 1)

    def act_part(act):
        if loads:
            act.wait_ge(loaded, 16 * PARTS)
        act.activation(w_parts[0][:, :, :], w[:, :, :], ACT.Copy).then_inc(high, 1)

    def dve_w(dve):
        dve.wait_ge(high, 1)
        nc.vector.tensor_tensor(w_parts[1][:, :, :], w[:, :, :], w_parts[0][:, :, :].bitcast(fp32),
                                ALU.subtract).then_inc(split, 1)

    def reduce(a):
        nc.vector.tensor_reduce(wa[:, :, S2 * a:S2 * a + H],
                                prod[:, KT * a:KT * a + KT, :].rearrange("p k (h d) -> p k h d", d=D),
                                AX.X, ALU.add).then_inc(wa_ready, 1)

    def dve_wa2(dve):
        if loads:
            dve.wait_ge(loaded, 16 * PARTS)
        product(nc.vector, 1, 0, KT).then_inc(wa_ready, 1)
        dve.wait_ge(products, 1)
        dve.wait_ge(wa_ready, 1)
        reduce(1)

    def dve_wa1(dve):
        dve.wait_ge(products, KT + 1)
        reduce(0)
        dve.wait_ge(wa_ready, 3)
        nc.vector.tensor_copy(wa_parts[:, :, 0, :], wa[:, :, :]).then_inc(split, 1)
        dve.wait_ge(split, 2)
        nc.vector.tensor_tensor(wa_parts[:, :, 1, :], wa[:, :, :], wa_parts[:, :, 0, :].bitcast(fp32),
                                ALU.subtract).then_inc(split, 1)

    return load, pool_part, act_part, dve_w, dve_wa2, dve_wa1, split


def first_transform(nc, tag, x_dram, adj_dram, w_dram, a_dram, v, mask, e_col, w, w_parts, a_bc, prod, wa, wa_parts,
                    xs, adj, adj_b, ident_b, deg, xn, h_parts, stats, mv, var_eps, half, rstd, sc, ident, ps, sem):
    H, D = 16, 32
    D1 = D + 1
    load_w, pool_w, act_w, dve_w, dve_wa2, dve_wa1, w_split = attention_vectors(
        nc, tag, H, D, 1, w, w_parts, a_bc, prod, wa, wa_parts, sem, loads=True)
    x_loaded = [sem(f"{tag}_x_loaded{k}") for k in range(4)]
    adj_loaded = [sem(f"{tag}_adj_loaded{k}") for k in range(4)]
    const = sem(tag + "_const")
    ln = [sem(tag + n) for n in ("_stats_ready", "_stats_seen", "_mean_ready", "_var_ready")]
    rstd_ready = sem(tag + "_rstd_ready")
    deg_ready = sem(tag + "_deg_ready")
    e_ready = sem(tag + "_e_ready")
    filled = sem(tag + "_filled")
    xn_ready = sem(tag + "_xn_ready")
    turned = sem(tag + "_turned")
    high_ready = sem(tag + "_high_ready")
    low_ready = sem(tag + "_low_ready")
    v_summed = sem(tag + "_v_summed")
    s_summed = sem(tag + "_s_summed")
    v_out = sem(tag + "_v_out")
    s_out = sem(tag + "_s_out")
    adj_turned = sem(tag + "_adj_turned")
    mask_dve = sem(tag + "_mask_dve")
    mask_act = sem(tag + "_mask_act")
    vh = v.rearrange("p t (h d) -> p t h d", d=D1)

    def run(eng, step):
        pipeline(eng, step, NT + 2, 4, NT, 4)

    with nc.Block() as block:

        @block.sync
        def _(sp):
            def step(s, k):
                if has_tile(s):
                    wait_from(sp, xn_ready, s - 3)
                    sp.dma_start(xs[:, k % 4, :], x_dram[rows(s), :]).then_inc(x_loaded[k % 4], 16)
                    wait_from(sp, deg_ready, s - 3)
                    sp.dma_start(adj[:, k % 4, :], adj_dram[rows(s), :]).then_inc(adj_loaded[k % 4], 16)
                if isinstance(s, int) and s == 0:
                    load_w(sp, w_dram, a_dram)
            run(sp, step)

        @block.gpsimd
        def _(pool):
            nc.gpsimd.memset(half[:, 0:1], -0.5).then_inc(const, 1)
            nc.gpsimd.memset(ident[:, :], 0.0).then_inc(const, 1)
            pool.wait_ge(const, 2)
            nc.gpsimd.affine_select(out=ident[:, :], in_=ident[:, :], compare_op=ALU.not_equal, fill=1.0,
                                    base=0, pattern=[[-1, P]], channel_multiplier=1).then_inc(const, 1)
            pool.wait_ge(const, 3)
            nc.gpsimd.tensor_copy(ident_b[:, :], ident[:, :]).then_inc(const, 1)
            nc.gpsimd.memset(vh[:, :, :, D:D1], 1.0).then_inc(const, 1)

            def step(s, k):
                if has_tile(s):
                    pool.wait_ge(ln[3], s + 1)
                    wait_from(pool, xn_ready, s - 1)
                    nc.gpsimd.tensor_tensor(rstd[:, k % 2, :], var_eps[:, k % 2, :], half[:, 0:1],
                                            ALU.pow).then_inc(rstd_ready, 1)
                if isinstance(s, int) and s == 0:
                    pool_w(pool)
            run(pool, step)

        @block.scalar
        def _(act):
            def copy_mask(t, q):
                act.wait_ge(adj_turned, 2 * t + q + 1)
                act.activation(mask[:, 8 * q:8 * q + 8, rows(t)],
                               ps[:, 6, :].bitcast(bf16).rearrange("p (j i) -> p j i", i=P),
                               ACT.Copy, scale=float(ONE8)).then_inc(mask_act, 1)

            def step(s, k):
                if has_tile(s):
                    act.wait_ge(adj_loaded[k % 4], 4 * (s - k % 4) + 16)
                    wait_from(act, e_ready, s - 1)
                    wait_from(act, adj_turned, 2 * s - 2)
                    act.activation(adj_b[:, k % 2, :], adj[:, k % 4, :], ACT.Copy,
                                   accum_out=deg[:, k % 2, :]).then_inc(deg_ready, 1)
                if has_tile(s - 1):
                    b = (k - 1) % 2
                    act.wait_ge(turned, s)
                    wait_from(act, s_summed, s - 2)
                    act.activation(h_parts[0][:, b, :, :], ps[:, b, :].rearrange("p (k i) -> p k i", i=P),
                                   ACT.Relu).then_inc(high_ready, 1)
                if isinstance(s, int) and s == 0:
                    act_w(act)
                if has_tile(s - 1):
                    copy_mask(s - 1, 0)
                if has_tile(s - 2):
                    act.wait_ge(v_summed, s - 1)
                    t = s - 2
                    dst = vh[:, t, :, 0:D] if isinstance(t, int) else (
                        vh[:, bass.ds(t, 1), :, 0:D].rearrange("p a h d -> p (a h) d"))
                    act.activation(dst, ps[:, 2 + k % 2, :].rearrange("p (h d) -> p h d", d=D),
                                   ACT.Copy).then_inc(v_out, 1)
            run(act, step)

        @block.vector
        def _(dve):
            def copy_mask(t, q):
                dve.wait_ge(adj_turned, 2 * t + q + 1)
                nc.vector.tensor_scalar(mask[:, 8 * q:8 * q + 8, rows(t)],
                                        ps[:, 7, :].bitcast(bf16).rearrange("p (j i) -> p j i", i=P),
                                        float(ONE8), None, ALU.mult).then_inc(mask_dve, 1)

            def step(s, k):
                if has_tile(s):
                    b = k % 2
                    dve.wait_ge(x_loaded[k % 4], 4 * (s - k % 4) + 16)
                    layer_norm_stats(nc, dve, xs[:, k % 4, :], b, stats, mv, var_eps, ln, s)
                if has_tile(s):
                    dve.wait_ge(deg_ready, s + 1)
                    e = e_col[:, s:s + 1] if isinstance(s, int) else e_col[:, bass.ds(s, 1)]
                    nc.vector.tensor_scalar(e, deg[:, b, :], 0.5, None, ALU.is_lt).then_inc(e_ready, 1)
                    dve.wait_ge(e_ready, s + 1)
                    nc.vector.tensor_scalar(adj_b[:, b, :], adj_b[:, b, :], e, None, ALU.add).then_inc(filled, 1)
                    dve.wait_ge(rstd_ready, s + 1)
                    wait_from(dve, turned, s - 1)
                    nc.vector.tensor_scalar(xn[:, b, :], xs[:, k % 4, :], mv[:, b, 0:1], rstd[:, b, :],
                                            ALU.subtract, ALU.mult).then_inc(xn_ready, 1)
                if has_tile(s - 1):
                    b = (k - 1) % 2
                    dve.wait_ge(high_ready, s)
                    nc.vector.scalar_tensor_tensor(
                        h_parts[1][:, b, :, :].rearrange("p k i -> p (k i)"), ps[:, b, :], 0.0,
                        h_parts[0][:, b, :, :].rearrange("p k i -> p (k i)").bitcast(fp32), ALU.max,
                        ALU.subtract).then_inc(low_ready, 1)
                if isinstance(s, int) and s == 0:
                    dve_wa2(dve)
                    dve_w(dve)
                if isinstance(s, int) and s == 1:
                    dve_wa1(dve)
                if has_tile(s - 1):
                    copy_mask(s - 1, 1)
                if has_tile(s - 2):
                    dve.wait_ge(s_summed, s - 1)
                    take_scores(nc, tile_of(sc, s - 2), ps[:, 4 + k % 2, :]).then_inc(s_out, 1)
            run(dve, step)

        @block.tensor
        def _(pe):
            pe.wait_ge(const, 5)

            def turn_adj(t, k, q):
                if q == 0:
                    pe.wait_ge(filled, t + 1)
                wait_from(pe, (mask_act, mask_dve)[q], t)
                for j in range(8):
                    last = nc.tensor.transpose(ps[:, 6 + q, :].bitcast(bf16)[:, rows(j)],
                                               adj_b[:, k % 2, rows(8 * q + j)], ident_b[:, :])
                last.then_inc(adj_turned, 1)

            def step(s, k):
                if has_tile(s - 1):
                    b = (k - 1) % 2
                    pe.wait_ge(xn_ready, s)
                    wait_from(pe, low_ready, s - 2)
                    for kt in range(KT):
                        last = nc.tensor.transpose(ps[:, b, rows(kt)], xn[:, b, rows(kt)], ident[:, :])
                    last.then_inc(turned, 1)
                    turn_adj(s - 1, k - 1, 0)
                if has_tile(s - 2):
                    b = k % 2
                    if isinstance(s, int) and s == 2:
                        pe.wait_ge(w_split, 3)
                    pe.wait_ge(low_ready, s - 1)
                    wait_from(pe, v_out, s - 3)
                    hs = [(h_parts[0][:, b, kt, :], h_parts[1][:, b, kt, :]) for kt in range(KT)]
                    split_matmul(nc, ps[:, 2 + b, :], hs,
                                 [(w_parts[0][:, kt, :], w_parts[1][:, kt, :]) for kt in range(KT)]
                                 ).then_inc(v_summed, 1)
                    wait_from(pe, s_out, s - 3)
                    score_matmul(nc, ps[:, 4 + b, :], hs, wa_parts).then_inc(s_summed, 1)
                if has_tile(s - 1):
                    turn_adj(s - 1, k - 1, 1)
            run(pe, step)


def middle(nc, tag, x_dram, x2_dram, v, out_w, out_parts, out_b, w, w_parts, a_bc, prod, wa, wa_parts, vt, a_parts,
           z, e, xs, xn, h_parts, stats, mv, var_eps, half, rstd, sc, v2, ident, ps, sem):
    H, D = 8, 64
    D1 = D + 1
    _, pool_w, act_w, dve_w, dve_wa2, dve_wa1, w_split = attention_vectors(
        nc, tag, H, D, H, w, w_parts, a_bc, prod, wa, wa_parts, sem, loads=False)
    x_loaded = [sem(f"{tag}_x_loaded{k}") for k in range(4)]
    stored = [sem(f"{tag}_stored{k}") for k in range(4)]
    const = sem(tag + "_const")
    ones_set = sem(tag + "_ones_set")
    out_high = sem(tag + "_out_high")
    out_split = sem(tag + "_out_split")
    staged = sem(tag + "_staged")
    a_turned = sem(tag + "_a_turned")
    a_high = sem(tag + "_a_high")
    a_low = sem(tag + "_a_low")
    summed = sem(tag + "_summed")
    z_ready = sem(tag + "_z_ready")
    exp_ready = sem(tag + "_exp_ready")
    elu_ready = sem(tag + "_elu_ready")
    x_ready = sem(tag + "_x_ready")
    ln = [sem(tag + n) for n in ("_stats_ready", "_stats_seen", "_mean_ready", "_var_ready")]
    rstd_ready = sem(tag + "_rstd_ready")
    xn_ready = sem(tag + "_xn_ready")
    turned = sem(tag + "_turned")
    high_ready = sem(tag + "_high_ready")
    low_ready = sem(tag + "_low_ready")
    v_summed = sem(tag + "_v_summed")
    s_summed = sem(tag + "_s_summed")
    v_out = sem(tag + "_v_out")
    s_out = sem(tag + "_s_out")
    vh = v2.rearrange("p t (h d) -> p t h d", d=D1)

    def run(eng, step):
        pipeline(eng, step, NT + 4, 4, NT, 4)

    with nc.Block() as block:

        @block.sync
        def _(sp):
            def step(s, k):
                if has_tile(s):
                    wait_from(sp, xn_ready, s - 3)
                    wait_from(sp, stored[k % 4], 4 * (s - k % 4))
                    sp.dma_start(xs[:, k % 4, :], x_dram[rows(s), :]).then_inc(x_loaded[k % 4], 16)
                if has_tile(s - 1):
                    sp.wait_ge(x_ready, s)
                    sp.dma_start(x2_dram[rows(s - 1), :], xs[:, (k - 1) % 4, :]).then_inc(stored[(k - 1) % 4], 16)
            run(sp, step)
            for k in range(4):
                sp.wait_ge(stored[k], 16 * NT // 4)

        @block.gpsimd
        def _(pool):
            def step(s, k):
                if has_tile(s):
                    wait_from(pool, a_turned, s - 1)
                    nc.gpsimd.tensor_copy(vt[:, k % 2, :], tile_of(v, s)[:, 0:F]).then_inc(staged, 1)
                if isinstance(s, int) and s == 2:
                    pool_w(pool)
                if has_tile(s - 3):
                    b = (k - 3) % 2
                    pool.wait_ge(ln[3], s - 2)
                    wait_from(pool, xn_ready, s - 3)
                    nc.gpsimd.tensor_tensor(rstd[:, b, :], var_eps[:, b, :], half[:, 0:1],
                                            ALU.pow).then_inc(rstd_ready, 1)
                if isinstance(s, int) and s == NT:
                    pool.wait_ge(staged, NT)
                    nc.gpsimd.memset(vh[:, :, :, D:D1], 1.0).then_inc(ones_set, 1)
            run(pool, step)

        @block.scalar
        def _(act):
            act.activation(out_parts[0][:, :, :], out_w[:, :, :], ACT.Copy).then_inc(out_high, 1)

            def step(s, k):
                if has_tile(s):
                    b = k % 2
                    act.wait_ge(a_turned, s + 1)
                    wait_from(act, summed, s - 1)
                    act.activation(a_parts[0][:, b, :, :], ps[:, 0, :].rearrange("p (k i) -> p k i", i=P),
                                   ACT.Copy).then_inc(a_high, 1)
                if isinstance(s, int) and s == 0:
                    act_w(act)
                if has_tile(s - 3):
                    b = (k - 3) % 2
                    act.wait_ge(turned, s - 2)
                    wait_from(act, s_summed, s - 4)
                    act.activation(h_parts[0][:, b, :, :], ps[:, 1, :].rearrange("p (k i) -> p k i", i=P),
                                   ACT.Relu).then_inc(high_ready, 1)
                if has_tile(s - 1):
                    b = (k - 1) % 2
                    act.wait_ge(z_ready, s)
                    wait_from(act, elu_ready, s - 2)
                    act.activation(e[:, b, :], z[:, b, :], ACT.Exp, bias=minus_one).then_inc(exp_ready, 1)
                if has_tile(s - 4):
                    act.wait_ge(v_summed, s - 3)
                    t = s - 4
                    dst = vh[:, t, :, 0:D] if isinstance(t, int) else (
                        vh[:, bass.ds(t, 1), :, 0:D].rearrange("p a h d -> p (a h) d"))
                    act.activation(dst, ps[:, 4 + k % 2, :].rearrange("p (h d) -> p h d", d=D),
                                   ACT.Copy).then_inc(v_out, 1)
            minus_one = half[:, 1:2]
            act.sem_inc(v_out, 2)
            act.wait_ge(const, 1)
            run(act, step)

        @block.vector
        def _(dve):
            dve.sem_inc(s_out, 2)
            nc.vector.memset(half[:, 1:2], -1.0).then_inc(const, 1)
            nc.vector.tensor_scalar(out_b[:, :], out_b[:, :], 1.0, None, ALU.add).then_inc(const, 1)
            dve.wait_ge(out_high, 1)
            nc.vector.tensor_tensor(out_parts[1][:, :, :], out_w[:, :, :], out_parts[0][:, :, :].bitcast(fp32),
                                    ALU.subtract).then_inc(out_split, 1)

            def step(s, k):
                if has_tile(s):
                    b = k % 2
                    dve.wait_ge(a_high, s + 1)
                    nc.vector.tensor_tensor(
                        a_parts[1][:, b, :, :].rearrange("p k i -> p (k i)"), ps[:, 0, :],
                        a_parts[0][:, b, :, :].rearrange("p k i -> p (k i)").bitcast(fp32),
                        ALU.subtract).then_inc(a_low, 1)
                if isinstance(s, int) and 1 <= s <= 3:
                    (dve_w, dve_wa2, dve_wa1)[s - 1](dve)
                if has_tile(s - 2):
                    b = k % 2
                    dve.wait_ge(rstd_ready, s - 1)
                    wait_from(dve, turned, s - 3)
                    nc.vector.tensor_scalar(xn[:, b, :], xs[:, (k - 2) % 4, :], mv[:, b, 0:1], rstd[:, b, :],
                                            ALU.subtract, ALU.mult).then_inc(xn_ready, 1)
                if has_tile(s - 1):
                    b = (k - 1) % 2
                    dve.wait_ge(summed, s)
                    wait_from(dve, x_ready, s - 2)
                    if isinstance(s, int) and s == 1:
                        dve.wait_ge(const, 2)
                    nc.vector.tensor_tensor(z[:, b, :], ps[:, 2 + b, :], out_b[:, :], ALU.add).then_inc(z_ready, 1)
                if has_tile(s - 3):
                    b = (k - 3) % 2
                    dve.wait_ge(high_ready, s - 2)
                    nc.vector.scalar_tensor_tensor(
                        h_parts[1][:, b, :, :].rearrange("p k i -> p (k i)"), ps[:, 1, :], 0.0,
                        h_parts[0][:, b, :, :].rearrange("p k i -> p (k i)").bitcast(fp32), ALU.max,
                        ALU.subtract).then_inc(low_ready, 1)
                if has_tile(s - 1):
                    b = (k - 1) % 2
                    xt = xs[:, (k - 1) % 4, :]
                    dve.wait_ge(exp_ready, s)
                    nc.vector.scalar_tensor_tensor(z[:, b, :], e[:, b, :], 1.0, z[:, b, :], ALU.min,
                                                   ALU.max).then_inc(elu_ready, 1)
                    dve.wait_ge(elu_ready, s)
                    dve.wait_ge(x_loaded[(k - 1) % 4], 4 * (s - 1 - (k - 1) % 4) + 16)
                    nc.vector.scalar_tensor_tensor(xt, z[:, b, :], -1.0, xt, ALU.add, ALU.add).then_inc(x_ready, 1)
                    dve.wait_ge(x_ready, s)
                    layer_norm_stats(nc, dve, xt, b, stats, mv, var_eps, ln, s - 1)
                if has_tile(s - 4):
                    dve.wait_ge(s_summed, s - 3)
                    take_scores(nc, tile_of(sc, s - 4), ps[:, 6 + k % 2, :]).then_inc(s_out, 1)
            run(dve, step)

        @block.tensor
        def _(pe):
            def step(s, k):
                if has_tile(s):
                    pe.wait_ge(staged, s + 1)
                    wait_from(pe, a_low, s)
                    for kt in range(KT):
                        last = nc.tensor.transpose(ps[:, 0, rows(kt)], vt[:, k % 2, rows(kt)], ident[:, :])
                    last.then_inc(a_turned, 1)
                if has_tile(s - 1):
                    b = (k - 1) % 2
                    if isinstance(s, int) and s == 1:
                        pe.wait_ge(out_split, 1)
                    pe.wait_ge(a_low, s)
                    wait_from(pe, z_ready, s - 2)
                    split_matmul(nc, ps[:, 2 + b, :],
                                 [(a_parts[0][:, b, kt, :], a_parts[1][:, b, kt, :]) for kt in range(KT)],
                                 [(out_parts[0][:, kt, :], out_parts[1][:, kt, :]) for kt in range(KT)]
                                 ).then_inc(summed, 1)
                if has_tile(s - 3):
                    b = (k - 3) % 2
                    pe.wait_ge(xn_ready, s - 2)
                    wait_from(pe, low_ready, s - 3)
                    for kt in range(KT):
                        last = nc.tensor.transpose(ps[:, 1, rows(kt)], xn[:, b, rows(kt)], ident[:, :])
                    last.then_inc(turned, 1)
                if has_tile(s - 4):
                    b = k % 2
                    if isinstance(s, int) and s == 4:
                        pe.wait_ge(w_split, 3)
                    pe.wait_ge(low_ready, s - 3)
                    wait_from(pe, v_out, s - 3)
                    hs = [(h_parts[0][:, b, kt, :], h_parts[1][:, b, kt, :]) for kt in range(KT)]
                    split_matmul(nc, ps[:, 4 + b, :], hs,
                                 [(w_parts[0][:, kt, :], w_parts[1][:, kt, :]) for kt in range(KT)]
                                 ).then_inc(v_summed, 1)
                    wait_from(pe, s_out, s - 3)
                    score_matmul(nc, ps[:, 6 + b, :], hs, wa_parts).then_inc(s_summed, 1)
            run(pe, step)


def mlp(nc, tag, x, x2_dram, out, raw, wT, b_rows, b_col, b4, v, enc_parts, o, o_parts, ident,
        ps, sem):
    CT = 4
    x_loaded = [sem(f"{tag}_x_loaded{c}") for c in range(4)]
    b_ready = sem(tag + "_b_ready")
    w_turned = sem(tag + "_w_turned")
    w_high = sem(tag + "_w_high")
    w_ready = sem(tag + "_w_ready")
    turned = sem(tag + "_turned")
    enc_high = sem(tag + "_enc_high")
    enc_low = sem(tag + "_enc_low")
    layer = [sem(f"{tag}_layer{n}") for n in (1, 2, 3)]
    high = [sem(f"{tag}_high{n}") for n in (1, 2, 3)]
    low = [sem(f"{tag}_low{n}") for n in (1, 2, 3)]
    l4 = sem(tag + "_l4")
    xb_ready = sem(tag + "_xb_ready")
    y_ready = sem(tag + "_y_ready")
    stored = sem(tag + "_stored")
    W1, W2, W3, W4 = 0, 1024, 1280, 1536
    HALVES = (2, 1, 2)
    BANK = ((2, 3), (4,), (6, 5))
    BIAS = (0, 2, 3)
    BANK4 = (5, 7)
    wH, wL = wT

    def w_at(start, n):
        return wH[:, start:start + n], wL[:, start:start + n]

    def schedule(c, enc, hidden, fourth):
        hidden(c, 0)
        for n in range(CT):
            enc(c + 1, n)
            fourth(c - 1, n)
            if n == 1:
                hidden(c, 1)
        hidden(c, 2)

    def run(enc, hidden, fourth):
        chunk = lambda f: lambda c, n: f(c, n) if 0 <= c < NT // CT else None
        for c in range(NT // CT + 1):
            schedule(c, chunk(lambda a, n: enc(CT * a + n)), chunk(hidden), chunk(lambda a, n: fourth(CT * a + n)))

    with nc.Block() as block:

        @block.sync
        def _(sp):
            for c in range(4):
                sp.dma_start(x[:, 4 * c:4 * c + 4, :],
                             x2_dram[c * 512:(c + 1) * 512, :].rearrange("(t p) f -> p t f", p=P)
                             ).then_inc(x_loaded[c], 16)
            for c in range(4):
                sp.wait_ge(y_ready, CT * (c + 1))
                sp.dma_start(out[c * 512:(c + 1) * 512, :].rearrange("(t p) f -> p t f", p=P),
                             x[:, 4 * c:4 * c + 4, :]).then_inc(stored, 16)
            sp.wait_ge(stored, 64)

        @block.gpsimd
        def _(pool):
            for c in range(4):
                pool.wait_ge(x_loaded[c], 16)
                nc.gpsimd.tensor_tensor(x[:, CT * c:CT * c + CT, :], x[:, CT * c:CT * c + CT, :],
                                        b4[:, :].unsqueeze(1).to_broadcast([P, CT, F]), ALU.add).then_inc(xb_ready, 1)

        @block.scalar
        def _(act):
            def enc(it):
                act.wait_ge(turned, it + 1)
                if it >= 8 and it % CT == 0:
                    act.wait_ge(layer[0], 2 * (it // CT - 1))
                act.activation(enc_parts[0][:, it // CT % 2, :, rows(it % CT)],
                               ps[:, it % 2, :].rearrange("p (k i) -> p k i", i=P), ACT.Copy).then_inc(enc_high, 1)

            def hidden(c, n):
                for h in range(HALVES[n]):
                    act.wait_ge(layer[n], HALVES[n] * c + h + 1)
                    if c:
                        act.wait_ge(low[n], HALVES[n] * (c - 1) + h + 1)
                        if h == 0:
                            act.wait_ge(*((layer[1], c), (layer[2], 2 * c), (l4, CT * c))[n])
                    bias = b_col[:, BIAS[n] + h:BIAS[n] + h + 1]
                    for to in (o[n], o_parts[n][0]):
                        act.activation(to[:, h, :], ps[:, BANK[n][h], :], ACT.Relu, bias=bias).then_inc(high[n], 1)

            for it in (0, 1):
                enc(it)
            for k in range(5):
                act.wait_ge(w_turned, k + 2)
                act.activation(wH[:, rows(k, F)], ps[:, 2 + k, :], ACT.Copy).then_inc(w_high, 1)
            for it in (2, 3):
                enc(it)
            act.wait_ge(b_ready, 1)
            run(enc, hidden, lambda it: None)

        @block.vector
        def _(dve):
            def enc(it):
                dve.wait_ge(enc_high, it + 1)
                at = (slice(None), it // CT % 2, slice(None), rows(it % CT))
                nc.vector.tensor_tensor(enc_parts[1][at], ps[:, it % 2, :].rearrange("p (k i) -> p k i", i=P),
                                        enc_parts[0][at].bitcast(fp32), ALU.subtract).then_inc(enc_low, 1)

            def hidden(c, n):
                for h in range(HALVES[n]):
                    dve.wait_ge(high[n], 2 * (HALVES[n] * c + h + 1))
                    nc.vector.tensor_tensor(o_parts[n][1][:, h, :], o[n][:, h, :], o_parts[n][0][:, h, :].bitcast(fp32),
                                            ALU.subtract).then_inc(low[n], 1)

            def fourth(it):
                dve.wait_ge(l4, it + 1)
                dve.wait_ge(xb_ready, it // CT + 1)
                nc.vector.tensor_tensor(x[:, it, :], ps[:, BANK4[it % 2], :], x[:, it, :], ALU.add).then_inc(y_ready, 1)

            dve.wait_ge(w_turned, 1)
            nc.vector.tensor_copy(b_col[:, :], ps[:, 7, 0:5]).then_inc(b_ready, 1)
            for it in (0, 1):
                enc(it)
            for k in range(5):
                dve.wait_ge(w_high, k + 1)
                nc.vector.tensor_tensor(wL[:, rows(k, F)], ps[:, 2 + k, :], wH[:, rows(k, F)].bitcast(fp32),
                                        ALU.subtract).then_inc(w_ready, 1)
            for it in (2, 3):
                enc(it)
            run(enc, hidden, fourth)

        @block.tensor
        def _(pe):
            def enc(it):
                if it >= 2:
                    pe.wait_ge(enc_low, it - 1)
                for k in range(KT):
                    last = nc.tensor.transpose(ps[:, it % 2, rows(k)], v[:, it, rows(k)], ident[:, :])
                last.then_inc(turned, 1)

            def hidden(c, n):
                if c == 0:
                    pe.wait_ge(w_ready, (2, 3, 5)[n])
                if n == 0:
                    pe.wait_ge(enc_low, CT * (c + 1))
                else:
                    pe.wait_ge(low[n - 1], HALVES[n - 1] * (c + 1))
                for h in range(HALVES[n]):
                    if c:
                        pe.wait_ge(high[n], 2 * (HALVES[n] * (c - 1) + h + 1))
                    if n == 2 and h == 1 and c:
                        pe.wait_ge(y_ready, CT * c - 1)
                    left = ([w_at(W1 + 256 * k + P * h, P) for k in range(KT)], [w_at(W2 + P * k, P) for k in range(2)],
                            [w_at(W3 + P * h, P)])[n]
                    right = ([(enc_parts[0][:, c % 2, k, :], enc_parts[1][:, c % 2, k, :]) for k in range(KT)] if n == 0
                             else [(o_parts[n - 1][0][:, k, :], o_parts[n - 1][1][:, k, :])
                                   for k in range(HALVES[n - 1])])
                    split_matmul(nc, ps[:, BANK[n][h], :], left, right).then_inc(layer[n], 1)

            def fourth(it):
                if it % CT == 0:
                    pe.wait_ge(low[2], 2 * (it // CT + 1))
                if it >= 2:
                    pe.wait_ge(y_ready, it - 1)
                if it % CT == 0:
                    pe.wait_ge(high[2], 4 * (it // CT + 1))
                split_matmul(nc, ps[:, BANK4[it % 2], :],
                             [(o_parts[2][0][:, k, rows(it % CT)], o_parts[2][1][:, k, rows(it % CT)])
                              for k in range(2)],
                             [w_at(W4 + 512 * k, F) for k in range(2)]).then_inc(l4, 1)

            for it in (0, 1):
                enc(it)
            nc.tensor.transpose(ps[:, 7, 0:5], b_rows[:, :], ident[0:5, 0:5]).then_inc(w_turned, 1)
            blocks = ([(W1 + 256 * k + P * h, 512 * h + P * k) for k in range(4) for h in range(2)]
                      + [(W2 + P * k, 1024 + P * k) for k in range(2)]
                      + [(W3 + P * h, 1280 + P * h) for h in range(2)]
                      + [(W4 + 512 * k + P * h, 1536 + 256 * h + P * k) for k in range(2) for h in range(4)])
            for n, (to, at) in enumerate(blocks):
                last = nc.tensor.transpose(ps[:, 2 + to // F, to % F:to % F + P], raw[:, at:at + P], ident[:, :])
                if n % 4 == 3:
                    last.then_inc(w_turned, 1)
            for it in (2, 3):
                enc(it)
            run(enc, hidden, fourth)


def build(nc, x, adj, w_seq, a1_0, a2_0, w_out, b_out, w_1, a1_1, a2_1, w1, b1, w2, b2, w3, b3, w4, b4, out):
    with ExitStack() as ctx:
        def sem(name):
            return ctx.enter_context(nc.semaphore(name))

        def allocator(stack, tag):
            return lambda name, shape, dt=fp32: stack.enter_context(nc.sbuf_tensor(f"{tag}{name}", shape, dt))

        keep = allocator(ctx, "")
        s1_rows = [nc.dram_tensor(f"s1_rows{n}", [h, N], fp32, kind="Internal").ap() for n, h in enumerate((16, 8))]
        x2_dram = nc.dram_tensor("x2", [N, F], fp32, kind="Internal").ap()
        ps = ctx.enter_context(nc.psum_tensor("ps", [P, 8, F], fp32))
        mask = keep("mask", [P, NT, N], u8)
        v = keep("v", [P, NT, 16 * 33])
        ident = keep("ident", [P, P])
        e_col = keep("e_col", [P, NT])
        half = keep("half", [P, 2])
        v0, v1 = v[:, :, 0:16 * 33], v[:, :, 0:8 * 65]
        sc = keep("sc", [P, NT, SC])
        mean = sc[:, :, :].rearrange("p t c -> p (t c)")

        s1 = keep("s1", [P, 2, N])
        raw = s1[:, :, :].rearrange("p b n -> p (b n)")
        raw, b_rows, b4_all = raw[:, 0:2560], raw[0:5, 2560:2560 + P], raw[:, 3072:3072 + F]
        late = [(raw[:, 0:1024].rearrange("p (o k) -> p o k", k=512), w1.rearrange("(o p) k -> p o k", p=P)),
                (raw[:, 1024:1280], w2),
                (raw[:, 1280:1536].rearrange("p (o k) -> p o k", k=128), w3.rearrange("(o p) k -> p o k", p=P)),
                (raw[:, 1536:2560].rearrange("p (o k) -> p o k", k=256), w4.rearrange("(o p) k -> p o k", p=P)),
                (b_rows[0:2, :], b1.rearrange("(o p) -> o p", p=P)), (b_rows[2:3, :], b2.rearrange("(o p) -> o p", p=P)),
                (b_rows[3:5, :], b3.rearrange("(o p) -> o p", p=P)), (b4_all, b4.partition_broadcast(P))]

        def transform_parts(own):
            return dict(
                w_parts=[own(f"w{n}", [P, KT, F], fp32r) for n in range(2)],
                prod=own("prod", [P, 2 * KT, F]), wa=own("wa", [P, KT, SC]),
                wa_parts=own("wa_parts", [P, KT, 2, SC], fp32r),
                xs=own("xs", [P, 4, F]), xn=own("xn", [P, 2, F]),
                h_parts=[own(f"h{n}", [P, 2, KT, P], fp32r) for n in range(2)],
                stats=own("stats", [P, 2, 6]), mv=own("mv", [P, 2, 2]), var_eps=own("var_eps", [P, 2, 1]),
                rstd=own("rstd", [P, 2, 1]))

        def attend(n, tag, H, D, UNITS, m_chunks, dve_tiles, first_dve_tiles, vv, **more):
            with ExitStack() as part:
                own = allocator(part, tag)
                MT = 2 * UNITS * len(m_chunks)
                small = [own("bd", [P, 2, NT, H]), own("ratio", [P, NT, H]), own("neg_s2", [P, NT, H])]
                sums = own("sums", [P, NT, 2 * (D + 1)])
                flat = sums[:, :, :].rearrange("p t c -> p (t c)")
                cut = lambda at: flat[:, at:at + NT * H].rearrange("p (t h) -> p t h", h=H)
                small += [cut(0), cut(NT * H), own("gm", [P, H + 1]), own("g", [P, H]),
                          own("shift", [P, 2, 2, NT]), own("one_minus_e", [P, NT])]
                s_rows = flat[:, 512:1024]
                if n:
                    more["mean_w"] = flat[:, 1024:1024 + P]
                attention(nc, tag, H, D, UNITS, m_chunks, dve_tiles, first_dve_tiles, mask, vv, sc, small, s_rows, s1_rows[n],
                          own("t_buf", [P, UNITS, NT, N // UNITS], u8),
                          own("u_buf", [P, UNITS, NT - MT, N // UNITS], u8),
                          s1, own("parts", [P, 2, 2 * NT + MT, D + 1, 3]), sums, ident, ps, sem, **more)

        with ExitStack() as part:
            own = allocator(part, "t_")
            first_transform(nc, "t", x, adj, [w_seq[rows(kt), :].rearrange("p (h d) -> p h d", d=32) for kt in range(KT)],
                            (a1_0, a2_0), v0, mask, e_col, w=own("w", [P, KT, F]), a_bc=own("a_bc", [P, 2, 32]),
                            adj=own("adj", [P, 4, N]), adj_b=own("adj_b", [P, 2, N], bf16),
                            ident_b=own("ident_b", [P, P], bf16), deg=own("deg", [P, 2, 1]),
                            half=half[:, 0:1], sc=sc, ident=ident, ps=ps, sem=sem, **transform_parts(own))
        with ExitStack() as part:
            own = allocator(part, "n_")
            out_w, out_b, w = own("out_w", [P, KT, F]), own("out_b", [P, F]), own("w", [P, KT, F])
            a_bc = own("a_bc", [P, 2, F])
            prefetch = [(out_w[:, :, :], w_out.rearrange("(k p) n -> p k n", p=P)),
                        (out_b[:, :], b_out.partition_broadcast(P)),
                        (a_bc[:, 0, :], a1_1.rearrange("h d -> (h d)").partition_broadcast(P)),
                        (a_bc[:, 1, :], a2_1.rearrange("h d -> (h d)").partition_broadcast(P))]
            prefetch += [(w[:, kt, :].rearrange("p (h d) -> p h d", d=64), w_1[:, rows(kt), :].rearrange("h p d -> p h d"))
                         for kt in range(KT)]
            attend(0, "a0", 16, 32, 1, (0, 2, 4, 6), (7, 15), (1, 3), v0, prefetch=prefetch)
            own = allocator(part, "m_")
            middle(nc, "m", x, x2_dram, v0, out_w, [own(f"out{n}", [P, KT, F], fp32r) for n in range(2)], out_b, w=w,
                   a_bc=a_bc, vt=own("vt", [P, 2, F]), a_parts=[own(f"a{n}", [P, 2, KT, P], fp32r) for n in range(2)],
                   z=own("z", [P, 2, F]), e=own("e", [P, 2, F]), half=half, sc=sc, v2=v1, ident=ident, ps=ps, sem=sem,
                   **transform_parts(own))
        attend(1, "a1", 8, 64, 2, (), (), (2, 3, 6, 7, 10, 11, 14), v1, e_col=e_col, mean=mean, prefetch_late=late)
        with ExitStack() as part:
            own = allocator(part, "p_")
            mlp(nc, "p", own("x", [P, NT, F]), x2_dram, out, raw, [own(f"wT{n}", [P, 2560], fp32r) for n in range(2)], b_rows,
                own("b_col", [P, 5]), b4_all, v1, [own(f"enc{n}", [P, 2, KT, F], fp32r) for n in range(2)],
                [own(f"o{n}", [P, (2, 1, 2)[n], F]) for n in range(3)],
                [[own(f"o{n}{m}", [P, (2, 1, 2)[n], F], fp32r) for m in range(2)] for n in range(3)], ident, ps, sem)


NAMES = ["x", "adj", "L0_gnn_W_seq", "L0_gnn_a1", "L0_gnn_a2", "L0_gnn_W_out", "L0_gnn_b_out", "L1_gnn_W",
         "L1_gnn_a1", "L1_gnn_a2", "L1_gnn_W1", "L1_gnn_b1", "L1_gnn_W2", "L1_gnn_b2", "L1_gnn_W3", "L1_gnn_b3",
         "L1_gnn_W4", "L1_gnn_b4"]


def kernel(**inputs):
    import numpy as np
    import concourse.bacc as bacc
    from concourse.bass_utils import run_bass_kernel_spmd

    nc = bacc.Bacc("TRN2", target_bir_lowering=False, num_devices=1)
    arrays, args = {}, []
    for name in NAMES:
        a = np.ascontiguousarray(inputs[name])
        arrays["in_" + name] = a
        args.append(nc.dram_tensor("in_" + name, a.shape, mybir.dt.from_np(a.dtype), kind="ExternalInput").ap())
    out = nc.dram_tensor("out_0", (N, F), fp32, kind="ExternalOutput").ap()
    build(nc, *args, out)
    r = run_bass_kernel_spmd(nc, [arrays], core_ids=[0])
    return r.results[0]["out_0"]
```
